# Optimizing a Trainium2 kernel written in Bass

```python
import numpy as np
import jax
import jax.numpy as jnp

def _softmax(x, axis=-1):
    return jax.nn.softmax(x, axis=axis)

def _gelu(x):
    return jax.nn.gelu(x, approximate=True)

def _silu(x):
    return jax.nn.silu(x)

def _sigmoid(x):
    return jax.nn.sigmoid(x)

def _layernorm(x, axis=-1, eps=1e-05):
    m = jnp.mean(x, axis=axis, keepdims=True)
    v = jnp.var(x, axis=axis, keepdims=True)
    return (x - m) / jnp.sqrt(v + eps)

def _scatter_add(tgt, idx, src, axis=0):
    return tgt.at[idx].add(src)

def _segment_sum(src, seg, n):
    return jax.ops.segment_sum(src, seg, n)
kernel_name = 'mk_xattn_ffn_d1_seqx_r4_c6fb13'

def setup_inputs(seed: int=0):
    np.random.seed(seed)
    _w = jnp.asarray

    def _rec_inputs():
        import jax
        import jax.numpy as jnp
        _rk = jax.random.key(seed)
        x = 7.22e-05 + 1 * jax.random.normal(jax.random.fold_in(_rk, 1), (4, 512, 256), jnp.float32)
        _lenS = 512 - jax.random.randint(jax.random.fold_in(_rk, 7), (4,), 0, max(1, 512 // 4) + 1, jnp.int32)
        _lenS2 = 1024 - jax.random.randint(jax.random.fold_in(_rk, 8), (4,), 0, max(1, 1024 // 4) + 1, jnp.int32)
        _ctx_1024P = jax.random.normal(jax.random.fold_in(_rk, 11), (4, 16, 256), jnp.float32)
        _ctx_1024c = jax.random.dirichlet(jax.random.fold_in(_rk, 511), 0.3 * jnp.ones((16,), jnp.float32), (4, 1024))
        _ctx_1024t = jnp.einsum('bsk,bkd->bsd', _ctx_1024c, _ctx_1024P)
        _ctx_1024t = _ctx_1024t * jax.lax.rsqrt(jnp.mean(jnp.square(_ctx_1024t)) + 1e-12) * 0.953939
        ctx_1024 = 4.13588e-05 + 0.999923 * (_ctx_1024t + 0.3 * jax.random.normal(jax.random.fold_in(_rk, 611), (4, 1024, 256), jnp.float32))
        return (x, ctx_1024)
    x, ctx_1024 = _rec_inputs()

    def _L0_xattn_setup():
        import jax, jax.numpy as jnp
        import numpy as np
        B, L, S, D, H = (4, 512, 512, 256, 16)
        E = D // H
        key = jax.random.key(seed)
        ks = jax.random.split(key, 7)
        sc = 1.0 / np.sqrt(D)
        return {'q': jax.random.normal(ks[0], (B, L, D), dtype=jnp.float32), 'k': jax.random.normal(ks[1], (B, S, D), dtype=jnp.float32), 'v': jax.random.normal(ks[2], (B, S, D), dtype=jnp.float32), 'Wq': jax.random.normal(ks[3], (D, D), dtype=jnp.float32) * sc, 'bq': jnp.zeros((D,), dtype=jnp.float32), 'Wo': jax.random.normal(ks[4], (D, D), dtype=jnp.float32) * sc, 'bo': jnp.zeros((D,), dtype=jnp.float32)}
    _L0_xattn_all = _L0_xattn_setup()
    _L0_xattn_in = {k: v for k, v in _L0_xattn_all.items() if k in ('Wq', 'bq', 'Wo', 'bo')}
    del _L0_xattn_all

    def _L0_ffn_setup():
        import jax, jax.numpy as jnp
        import numpy as np
        B, S, D, DO = (4, 512, 256, 256)
        E, K = (20, 2)
        key = jax.random.key(seed)
        ks = jax.random.split(key, 6)
        sc_d = 1.0 / np.sqrt(D)
        sc_h = 1.0 / np.sqrt(D // 4)
        return {'x': jax.random.normal(ks[0], (B, S, D), jnp.float32), 'wg1': jax.random.normal(ks[1], (D, D // 4), jnp.float32) * sc_d, 'bg1': jnp.zeros((D // 4,), jnp.float32), 'wg2': jax.random.normal(ks[2], (D // 4, 2 * E), jnp.float32) * sc_h, 'bg2': jnp.zeros((2 * E,), jnp.float32), 'We': jax.random.normal(ks[3], (E, D, DO), jnp.float32) * sc_d, 'be': jnp.zeros((E, DO), jnp.float32)}
    _L0_ffn_all = _L0_ffn_setup()
    _L0_ffn_in = {k: v for k, v in _L0_ffn_all.items() if k in ('wg1', 'bg1', 'wg2', 'bg2', 'We', 'be')}
    del _L0_ffn_all
    return {'x': x, 'ctx_1024': ctx_1024, 'L0_xattn_Wq': _L0_xattn_in['Wq'], 'L0_xattn_bq': _L0_xattn_in['bq'], 'L0_xattn_Wo': _L0_xattn_in['Wo'], 'L0_xattn_bo': _L0_xattn_in['bo'], 'L0_ffn_wg1': _L0_ffn_in['wg1'], 'L0_ffn_bg1': _L0_ffn_in['bg1'], 'L0_ffn_wg2': _L0_ffn_in['wg2'], 'L0_ffn_bg2': _L0_ffn_in['bg2'], 'L0_ffn_We': _L0_ffn_in['We'], 'L0_ffn_be': _L0_ffn_in['be']}

def reference(x, ctx_1024, L0_xattn_Wq, L0_xattn_bq, L0_xattn_Wo, L0_xattn_bo, L0_ffn_wg1, L0_ffn_bg1, L0_ffn_wg2, L0_ffn_bg2, L0_ffn_We, L0_ffn_be):
    import jax
    import jax.numpy as jnp

    def _L0_xattn_ref(q, k, v, Wq, bq, Wo, bo):
        import jax, jax.numpy as jnp
        import numpy as np
        B, L, S, D, H = (4, 512, 512, 256, 16)
        E = D // H
        b, l, _ = q.shape
        s = k.shape[1]
        qp = (q @ Wq.T + bq).reshape(b, l, H, E)
        kp = (k @ Wq.T + bq).reshape(b, s, H, E)
        vp = (v @ Wq.T + bq).reshape(b, s, H, E)
        scale = 1.0 / np.sqrt(E)
        scores = jnp.einsum('blhe,bshe->bhls', qp, kp)
        attn = jax.nn.softmax(scale * scores, axis=-1)
        out = jnp.einsum('bhls,bshd->blhd', attn, vp)
        out = jnp.transpose(out, (0, 2, 1, 3)).reshape(b, l, H * E)
        return out @ Wo.T + bo

    def _L0_ffn_ref(x, wg1, bg1, wg2, bg2, We, be):
        import jax, jax.numpy as jnp
        import numpy as np
        B, S, D, DO = (4, 512, 256, 256)
        E, K = (20, 2)
        Bv, Sv, Dv = x.shape
        xf = x.reshape(-1, Dv)
        h = jax.nn.gelu(xf @ wg1 + bg1, approximate=False)
        logits = (xf @ 0.0 + (h @ wg2 + bg2))[:, :E] if False else (h @ wg2 + bg2)[:, :E]
        probs = jax.nn.softmax(logits, axis=-1)
        top_vals, top_idx = jax.lax.top_k(probs, K)
        N = xf.shape[0]
        gates = jnp.zeros((N, E), xf.dtype).at[jnp.arange(N)[:, None], top_idx].set(top_vals)

        def body(y, eb):
            We_e, be_e, g_e = eb
            return (y + g_e[:, None] * (xf @ We_e + be_e), None)
        y0 = jnp.zeros((N, be.shape[-1]), xf.dtype)
        y, _ = jax.lax.scan(body, y0, (We, be, gates.T))
        return y.reshape(Bv, Sv, -1)
    x = x + _L0_xattn_ref(_layernorm(x, axis=-1), ctx_1024, ctx_1024, L0_xattn_Wq, L0_xattn_bq, L0_xattn_Wo, L0_xattn_bo)
    x = x + _L0_ffn_ref(_layernorm(x, axis=-1), L0_ffn_wg1, L0_ffn_bg1, L0_ffn_wg2, L0_ffn_bg2, L0_ffn_We, L0_ffn_be)
    return x

_drawn_inputs = setup_inputs


def setup_inputs(seed=0):
    import zlib

    import numpy as np

    out = dict(_drawn_inputs(seed))
    spreads = {'L0_xattn_bq': (0.0, 0.1),
     'L0_xattn_bo': (0.0, 0.1),
     'L0_ffn_bg1': (0.0, 0.1),
     'L0_ffn_bg2': (0.0, 0.1),
     'L0_ffn_be': (0.0, 0.478)}
    factors = {}
    for name, (base, spread) in spreads.items():
        noise = np.random.default_rng([zlib.crc32(name.encode()), seed]).standard_normal(out[name].shape)
        drawn = base * np.exp(spread * noise) if base else spread * noise
        out[name] = jnp.asarray(drawn.astype(out[name].dtype))
    for name, factor in factors.items():
        out[name] = (out[name] * factor).astype(out[name].dtype)
    return out
```

```python
from contextlib import ExitStack

import concourse.bass as bass
from concourse import mybir

ALU = mybir.AluOpType
ACT = mybir.ActivationFunctionType
AX_X = mybir.AxisListType.X
F32 = mybir.dt.float32
F32R = mybir.dt.float32r
U32 = mybir.dt.uint32

P = 128
B, L, S, D = 4, 512, 1024, 256
H = 16
E = D // H
KC = D // P
NX = 20
HID = D // 4
GH = 4
NG = H // GH
LT = L // P
ST = S // P
NT = B * LT
SCALE = float(E) ** -0.5
EPS = 1e-5
VW = E + 1
PAIRS = NX // 2
RAW = 4

Q_SLABS = (0, 0, 1)
K_SLABS = (0, 1, 0)
MROW = 3 * E
HI, LO = 0, 1


def wait(eng, sem, value):
    if not isinstance(value, int) or value > 0:
        eng.wait_ge(sem, value)


def mixed_kernel(nc, x, ctx_in, wq, bq, wo, bo, wg1, bg1, wg2, bg2, we, be, out):
    q_parts = nc.dram_tensor("q_parts", [B, 2, NG, GH, E, L], F32, kind="Internal").ap()
    k_parts = nc.dram_tensor("k_parts", [B, 2, NG, GH, E, S], F32, kind="Internal").ap()
    attn_rows = nc.dram_tensor("attn_rows", [B, L, D], F32, kind="Internal").ap()
    v_parts = nc.dram_tensor("v_parts", [B, NG, P, ST, GH * VW], F32, kind="Internal").ap()

    with ExitStack() as whole:
        def kept(name, shape, dt):
            return whole.enter_context(nc.sbuf_tensor(name, shape, dt))

        psum = whole.enter_context(nc.psum_tensor("psum", [P, 8, 512], F32))
        ident = kept("ident", [P, P], F32)
        wo_t = kept("wo_t", [P, 2, KC, D], F32R)
        wg1_t = kept("wg1_t", [P, 2, KC, P], F32R)
        w_raw = kept("w_raw", [P, RAW, KC, 2, D], F32)
        raw_loaded = [whole.enter_context(nc.semaphore(f"raw_loaded{i}")) for i in range(RAW)]
        with nc.sbuf_tensor("q_stack", [P, NG, GH, L], F32R) as q_stack, \
                nc.sbuf_tensor("k_stack", [P, NG, GH, S], F32R) as k_stack:
            project(nc, psum, ident, wo_t, wg1_t, w_raw, raw_loaded, q_stack, k_stack, x, ctx_in, wq, bq, wo, wg1,
                    we, q_parts, k_parts, v_parts)
            attend(nc, psum, ident, q_stack, k_stack, q_parts, k_parts, v_parts, attn_rows)
        feed_forward(nc, psum, ident, wo_t, wg1_t, attn_rows, w_raw, raw_loaded, x, bo, bg1, wg2, bg2, we, be, out)


def load_pair(sp, we, w_raw, raw_loaded, p):
    for i in range(2):
        sp.dma_start(w_raw[:, p % RAW, :, i, :], we[2 * p + i].rearrange("(k p) o -> p k o", p=P)).then_inc(
            raw_loaded[p % RAW], 16)


def project(nc, psum, ident, wo_t, wg1_t, w_raw, raw_loaded, q_stack, k_stack, x, ctx_in, wq, bq, wo, wg1, we,
            q_parts, k_parts, v_parts):
    TILES = LT
    CHUNKS = 1 + S // L
    with ExitStack() as ctx:
        def sb(name, shape, dt):
            return ctx.enter_context(nc.sbuf_tensor(name, shape, dt))

        def sem(name):
            return ctx.enter_context(nc.semaphore(name))

        w_nat = sb("w_nat", [P, 2, KC, D], F32)
        g_nat = sb("g_nat", [P, KC, P], F32)
        wq_t = sb("wq_t", [P, 2, KC, D], F32R)
        bq_col = sb("bq_col", [P, KC], F32)
        bq_row = sb("bq_row", [P, D], F32)
        x_in = sb("x_in", [P, TILES, D], F32)
        c_in = [sb(f"c_in{i}", [P, TILES, D], F32) for i in range(CHUNKS - 1)]
        x_norm = sb("x_norm", [P, TILES, D], F32)
        stats = sb("stats", [P, TILES, 6], F32)
        mean_gap = sb("mean_gap", [P, TILES], F32)
        squares = sb("squares", [P, TILES], F32)
        gap_square = sb("gap_square", [P, TILES], F32)
        mean = sb("mean", [P, TILES], F32)
        var = sb("var", [P, TILES], F32)
        var_eps = sb("var_eps", [P, TILES], F32)
        minus_half = sb("minus_half", [P, TILES], F32)
        rstd = sb("rstd", [P, TILES], F32)
        tok_t = [sb(f"tok_t{i}", [P, 2, KC, L], F32R) for i in range(CHUNKS)]
        stage = [sb(f"stage{c}", [P, 2, L], F32R) for c in range(KC)]
        v_stage = [sb(f"v_stage{i}", [P, NG, TILES, GH * VW], F32) for i in range(CHUNKS - 1)]

        consts_loaded = sem("consts_loaded")
        g_zeroed = sem("g_zeroed")
        g_loaded = sem("g_loaded")
        ident_zeroed = sem("ident_zeroed")
        ident_ready = sem("ident_ready")
        filled = sem("filled")
        wt_done = sem("wt_done")
        wt_hi = sem("wt_hi")
        wt_lo = sem("wt_lo")
        x_loaded = sem("x_loaded")
        c_loaded = [sem(f"c_loaded{i}") for i in range(CHUNKS - 1)]
        stats_done = sem("stats_done")
        gap_done = sem("gap_done")
        squares_done = sem("squares_done")
        mean_ready = sem("mean_ready")
        square_done = sem("square_done")
        var_done = sem("var_done")
        eps_added = sem("eps_added")
        rstd_ready = sem("rstd_ready")
        norm_ready = sem("norm_ready")
        tok_done = sem("tok_done")
        tok_hi = sem("tok_hi")
        tok_lo = sem("tok_lo")
        proj_done = sem("proj_done")
        proj_hi = sem("proj_hi")
        proj_lo = sem("proj_lo")
        stored = [sem(f"stored{c}") for c in range(KC)]
        v_done = sem("v_done")
        v_ready = sem("v_ready")
        v_stored = [sem(f"v_stored{i}") for i in range(CHUNKS - 1)]

        NTR = CHUNKS * KC
        NV = (CHUNKS - 1) * 2

        block = ctx.enter_context(nc.Block())

        @block.sync
        def _(sp):
            sp.dma_start(w_nat[:, 0], wq.rearrange("(c p) i -> p c i", p=P)).then_inc(consts_loaded, 16)
            sp.dma_start(w_nat[:, 1], wo.rearrange("(c p) i -> p c i", p=P)).then_inc(consts_loaded, 16)
            sp.dma_start(bq_col[:], bq.rearrange("(c p) -> p c", p=P),
                         allow_slow_non_contiguous=True).then_inc(consts_loaded, 16)
            sp.dma_start(bq_row[:], bq.partition_broadcast(P)).then_inc(consts_loaded, 16)
            sp.wait_ge(g_zeroed, 1)
            sp.dma_start(g_nat[:, :, 0:HID], wg1.rearrange("(k p) h -> p k h", p=P)).then_inc(g_loaded, 16)

            def batch(b):
                for n in range(CHUNKS):
                    for c in range(KC):
                        sp.wait_ge(proj_lo, NTR * b + KC * n + c + 1)
                        for part in range(2):
                            src = stage[c][:, part, :].bitcast(F32)
                            if n == 0:
                                dst = q_parts[b, part].rearrange("g j e l -> (g j e) l")[c * P:(c + 1) * P, :]
                            else:
                                dst = k_parts[b, part].rearrange("g j e l -> (g j e) l")[
                                    c * P:(c + 1) * P, (n - 1) * L:n * L]
                            sp.dma_start(dst, src).then_inc(stored[c], 16)
                    if n > 0:
                        i = n - 1
                        sp.wait_ge(v_ready, 2 * TILES * b + TILES * n)
                        dst = v_parts[b, :, :, i * TILES:(i + 1) * TILES, :].rearrange("g p t v -> p g t v")
                        sp.dma_start(dst, v_stage[i][:]).then_inc(v_stored[i], 16)

            batch(0)
            with sp.Fori(1, B) as b:
                batch(b)
            for c in range(KC):
                sp.wait_ge(stored[c], 2 * 16 * CHUNKS * B)
            for i in range(CHUNKS - 1):
                sp.wait_ge(v_stored[i], 16 * B)
            for p in range(RAW):
                load_pair(sp, we, w_raw, raw_loaded, p)

        @block.gpsimd
        def _(pool):
            nc.gpsimd.memset(g_nat[:], 0.0).then_inc(g_zeroed, 1)
            nc.gpsimd.memset(ident[:], 0.0).then_inc(ident_zeroed, 1)
            nc.gpsimd.memset(minus_half[:], -0.5).then_inc(filled, 1)
            for i in range(CHUNKS - 1):
                nc.gpsimd.memset(v_stage[i][:], 1.0).then_inc(filled, 1)
            pool.wait_ge(ident_zeroed, 1)
            nc.gpsimd.affine_select(out=ident[:], in_=ident[:], compare_op=ALU.not_equal, fill=1.0, base=0,
                                    pattern=[[-1, P]], channel_multiplier=1).then_inc(ident_ready, 1)
            pool.wait_ge(filled, 1)
            def batch(b):
                wait(pool, norm_ready, TILES * b)
                pool.dma_start(x_in[:], x[b].rearrange("(t p) d -> p t d", p=P)).then_inc(x_loaded, 16)
                wait(pool, tok_done, NTR * b)
                for i in range(CHUNKS - 1):
                    src = ctx_in[b, i * L:(i + 1) * L, :].rearrange("(t p) d -> p t d", p=P)
                    pool.dma_start(c_in[i][:], src).then_inc(c_loaded[i], 16)
                pool.wait_ge(eps_added, b + 1)
                nc.gpsimd.tensor_tensor(rstd[:], var_eps[:], minus_half[:], ALU.pow).then_inc(rstd_ready, 1)

            batch(0)
            with pool.Fori(1, B) as b:
                batch(b)
            nc.gpsimd.memset(q_stack[:].bitcast(F32), 0.0)
            nc.gpsimd.memset(k_stack[:].bitcast(F32), 0.0)

        @block.vector
        def _(dve):
            for n, (dst, bank) in enumerate(((wq_t, 0), (wo_t, 1))):
                dve.wait_ge(wt_hi, n + 1)
                src = psum[:, bank, :].rearrange("p (k o) -> p k o", k=KC)
                nc.vector.tensor_tensor(dst[:, LO], src, dst[:, HI].bitcast(F32), ALU.subtract).then_inc(wt_lo, 1)
            dve.wait_ge(wt_hi, 3)
            nc.vector.tensor_tensor(wg1_t[:, LO], g_nat[:], wg1_t[:, HI].bitcast(F32),
                                    ALU.subtract).then_inc(wt_lo, 1)
            dve.wait_ge(consts_loaded, 64)
            dve.wait_ge(filled, CHUNKS)

            def split_tok(b, n):
                for k in range(KC):
                    dve.wait_ge(tok_hi, NTR * b + KC * n + k + 1)
                    nc.vector.tensor_tensor(tok_t[n][:, LO, k, :], psum[:, k, :], tok_t[n][:, HI, k, :].bitcast(F32),
                                            ALU.subtract).then_inc(tok_lo, 1)

            def split_proj(b, n):
                for c in range(KC):
                    dve.wait_ge(proj_hi, NTR * b + KC * n + c + 1)
                    nc.vector.scalar_tensor_tensor(
                        out=stage[c][:, LO, :], in0=psum[:, 2 + c, :], scalar=bq_col[:, c:c + 1],
                        in1=stage[c][:, HI, :].bitcast(F32), op0=ALU.add, op1=ALU.subtract).then_inc(proj_lo, 1)

            def batch(b):
                dve.wait_ge(x_loaded, 16 * (b + 1))
                for t in range(TILES):
                    nc.vector.bn_stats(stats[:, t, :], x_in[:, t, :]).then_inc(stats_done, 1)
                dve.wait_ge(stats_done, TILES * (b + 1))
                nc.vector.tensor_tensor(mean_gap[:], stats[:, :, 1], stats[:, :, 4], ALU.subtract).then_inc(gap_done, 1)
                nc.vector.tensor_tensor(squares[:], stats[:, :, 2], stats[:, :, 5], ALU.add).then_inc(squares_done, 1)
                dve.wait_ge(gap_done, b + 1)
                nc.vector.scalar_tensor_tensor(out=mean[:], in0=mean_gap[:], scalar=-0.5, in1=stats[:, :, 1],
                                               op0=ALU.mult, op1=ALU.add).then_inc(mean_ready, 1)
                nc.vector.scalar_tensor_tensor(out=gap_square[:], in0=mean_gap[:], scalar=0.25, in1=mean_gap[:],
                                               op0=ALU.mult, op1=ALU.mult).then_inc(square_done, 1)
                dve.wait_ge(squares_done, b + 1)
                dve.wait_ge(square_done, b + 1)
                nc.vector.scalar_tensor_tensor(out=var[:], in0=squares[:], scalar=1.0 / D, in1=gap_square[:],
                                               op0=ALU.mult, op1=ALU.add).then_inc(var_done, 1)
                dve.wait_ge(var_done, b + 1)
                nc.vector.tensor_scalar(var_eps[:], var[:], EPS, None, ALU.add).then_inc(eps_added, 1)
                dve.wait_ge(mean_ready, b + 1)
                dve.wait_ge(rstd_ready, b + 1)
                wait(dve, tok_done, NTR * b)
                for t in range(TILES):
                    nc.vector.tensor_scalar(x_norm[:, t, :], x_in[:, t, :], mean[:, t:t + 1], rstd[:, t:t + 1],
                                            ALU.subtract, ALU.mult).then_inc(norm_ready, 1)
                split_tok(b, 0)
                for n in range(CHUNKS):
                    if n + 1 < CHUNKS:
                        split_tok(b, n + 1)
                    split_proj(b, n)
                    if n > 0:
                        i = n - 1
                        wait(dve, v_stored[i], 16 * b)
                        for t in range(TILES):
                            dve.wait_ge(v_done, NV * b + 2 * i + t // 2 + 1)
                            dst = v_stage[i][:, :, t, :].rearrange("p g (j v) -> p g j v", j=GH)[:, :, :, 0:E]
                            src = psum[:, 4 + t // 2, (t % 2) * D:(t % 2 + 1) * D]
                            nc.vector.tensor_tensor(
                                dst, src.rearrange("p (g j e) -> p g j e", g=NG, j=GH),
                                bq_row[:].rearrange("p (g j e) -> p g j e", g=NG, j=GH), ALU.add).then_inc(v_ready, 1)

            batch(0)
            with dve.Fori(1, B) as b:
                batch(b)
        @block.scalar
        def _(act):
            for n, (dst, bank) in enumerate(((wq_t, 0), (wo_t, 1))):
                act.wait_ge(wt_done, n + 1)
                src = psum[:, bank, :].rearrange("p (k o) -> p k o", k=KC)
                nc.scalar.activation(dst[:, HI], src, ACT.Copy).then_inc(wt_hi, 1)
            act.wait_ge(g_loaded, 16)
            nc.scalar.activation(wg1_t[:, HI], g_nat[:], ACT.Copy).then_inc(wt_hi, 1)
            act.wait_ge(consts_loaded, 64)

            def round_tok(b, n):
                for k in range(KC):
                    act.wait_ge(tok_done, NTR * b + KC * n + k + 1)
                    nc.scalar.activation(tok_t[n][:, HI, k, :], psum[:, k, :], ACT.Copy).then_inc(tok_hi, 1)

            def round_proj(b, n):
                for c in range(KC):
                    act.wait_ge(proj_done, NTR * b + KC * n + c + 1)
                    wait(act, stored[c], 2 * 16 * (CHUNKS * b + n))
                    nc.scalar.activation(stage[c][:, HI, :], psum[:, 2 + c, :], ACT.Identity,
                                         bias=bq_col[:, c:c + 1]).then_inc(proj_hi, 1)

            def batch(b):
                round_tok(b, 0)
                for n in range(CHUNKS):
                    if n + 1 < CHUNKS:
                        round_tok(b, n + 1)
                    round_proj(b, n)

            batch(0)
            with act.Fori(1, B) as b:
                batch(b)
        @block.tensor
        def _(pe):
            pe.wait_ge(ident_ready, 1)
            pe.wait_ge(consts_loaded, 64)
            for n in range(2):
                for k in range(KC):
                    for c in range(KC):
                        last = nc.tensor.transpose(psum[:, n, k * D + c * P:k * D + (c + 1) * P],
                                                   w_nat[:, n, c, k * P:(k + 1) * P], ident[:])
                last.then_inc(wt_done, 1)
            pe.wait_ge(wt_lo, 3)

            def transposes(b, n):
                if n == 0:
                    pe.wait_ge(norm_ready, TILES * (b + 1))
                    src = x_norm
                else:
                    pe.wait_ge(c_loaded[n - 1], 16 * (b + 1))
                    src = c_in[n - 1]
                wait(pe, tok_lo, NTR * b + KC * n)
                for k in range(KC):
                    for t in range(TILES):
                        last = nc.tensor.transpose(psum[:, k, t * P:(t + 1) * P], src[:, t, k * P:(k + 1) * P],
                                                   ident[:])
                    last.then_inc(tok_done, 1)

            def projections(b, n):
                pe.wait_ge(tok_lo, NTR * b + KC * (n + 1))
                for c in range(KC):
                    wait(pe, proj_lo, NTR * b + (KC * n + c - 1 if KC * n + c > 1 else 0))
                    terms = [(HI, HI, k) for k in range(KC)] + [(LO, HI, k) for k in range(KC)] + [
                        (HI, LO, k) for k in range(KC)]
                    for m, (a, w, k) in enumerate(terms):
                        last = nc.tensor.matmul(psum[:, 2 + c, :], wq_t[:, w, k, c * P:(c + 1) * P],
                                                tok_t[n][:, a, k, :], start=(m == 0), stop=(m == len(terms) - 1))
                    last.then_inc(proj_done, 1)

            def values(b, i):
                for pr in range(2):
                    w = 2 * i + pr
                    wait(pe, v_ready, 2 * TILES * b + (2 * (w - 1) if w > 1 else 0))
                    for h in range(2):
                        t = 2 * pr + h
                        terms = [(HI, HI, k) for k in range(KC)] + [(LO, HI, k) for k in range(KC)] + [
                            (HI, LO, k) for k in range(KC)]
                        for m, (a, w, k) in enumerate(terms):
                            last = nc.tensor.matmul(psum[:, 4 + pr, h * D:(h + 1) * D],
                                                    tok_t[i + 1][:, a, k, t * P:(t + 1) * P], wq_t[:, w, k, :],
                                                    start=(m == 0), stop=(m == len(terms) - 1))
                    last.then_inc(v_done, 1)

            def batch(b):
                transposes(b, 0)
                for n in range(CHUNKS):
                    if n + 1 < CHUNKS:
                        transposes(b, n + 1)
                    projections(b, n)
                    if n > 0:
                        values(b, n - 1)

            batch(0)
            with pe.Fori(1, B) as b:
                batch(b)
def attend(nc, psum, ident, q_stack, k_stack, q_parts, k_parts, v_parts, attn_rows):
    SLOTS = NG
    ITEMS = LT * GH * 2
    with ExitStack() as ctx:
        def sb(name, shape, dt):
            return ctx.enter_context(nc.sbuf_tensor(name, shape, dt))

        def sem(name):
            return ctx.enter_context(nc.semaphore(name))

        v_stack = sb("v_stack", [P, SLOTS, ST, GH * VW], F32)
        probs = sb("probs", [P, 2, GH, L], F32)
        max_part = sb("max_part", [P, 2, LT, GH, 2], F32)
        neg_max = sb("neg_max", [P, LT, GH], F32)
        max_split = sb("max_split", [P, LT, 2, GH], F32R)
        max_rows = sb("max_rows", [2 * GH, L], F32)
        zero_rows = sb("zero_rows", [2, GH * L], F32)
        one_rows = sb("one_rows", [2, GH * S], F32)
        o_raw = sb("o_raw", [P, L], F32)
        recip = sb("recip", [P, LT, GH], F32)
        attn_out = sb("attn_out", [P, 2, GH, LT, E], F32)

        cleared = sem("cleared")
        ones_set = sem("ones_set")
        stack_loaded = [sem(f"stack_loaded{i}") for i in range(SLOTS)]
        scores_done = sem("scores_done")
        scores_read = sem("scores_read")
        max_ready = sem("max_ready")
        hi_ready = sem("hi_ready")
        split_ready = sem("split_ready")
        max_turned = sem("max_turned")
        max_copied = sem("max_copied")
        max_placed = sem("max_placed")
        keyed_done = sem("keyed_done")
        exp_done = sem("exp_done")
        out_done = sem("out_done")
        out_copied = sem("out_copied")
        out_turned = sem("out_turned")
        recip_ready = sem("recip_ready")
        out_ready = sem("out_ready")
        attn_stored = [sem(f"attn_stored{i}") for i in range(2)]

        KEYED, MAXB, OUTB, TURN = 0, 4, 6, 7
        LOADS = 2 * len(Q_SLABS) + 2

        block = ctx.enter_context(nc.Block())

        @block.gpsimd
        def _(pool):
            nc.gpsimd.memset(zero_rows[:], 0.0).then_inc(cleared, 1)
            nc.gpsimd.memset(one_rows[:], 1.0).then_inc(cleared, 1)

        @block.sync
        def _(sp):
            def load(b, g):
                for r, part in enumerate(Q_SLABS):
                    sp.dma_start(q_stack[r * E:(r + 1) * E, g, :, :].bitcast(F32),
                                 q_parts[b, part, g].rearrange("j e l -> e j l")).then_inc(stack_loaded[g], 16)
                for r, part in enumerate(K_SLABS):
                    sp.dma_start(k_stack[r * E:(r + 1) * E, g, :, :].bitcast(F32),
                                 k_parts[b, part, g].rearrange("j e s -> e j s")).then_inc(stack_loaded[g], 16)
                sp.dma_start(q_stack[MROW:MROW + 2, g, :, :].bitcast(F32),
                             zero_rows[:].rearrange("p (j l) -> p j l", j=GH)).then_inc(stack_loaded[g], 16)
                sp.dma_start(v_stack[:, g, :, :], v_parts[b, g]).then_inc(stack_loaded[g], 16)

            def place_max(count, g):
                sp.wait_ge(max_copied, count)
                for part in range(2):
                    sp.dma_start(q_stack[MROW + part:MROW + part + 1, g, :, :].bitcast(F32),
                                 max_rows[part * GH:(part + 1) * GH, :]).then_inc(max_placed, 16)

            sp.wait_ge(cleared, 2)
            for g in range(SLOTS):
                sp.dma_start(k_stack[MROW:MROW + 2, g, :, :].bitcast(F32),
                             one_rows[:].rearrange("p (j s) -> p j s", j=GH)).then_inc(ones_set, 16)
            for g in range(SLOTS):
                load(0, g)
            place_max(1, 0)

            def batch(b, last):
                for g in range(NG):
                    if not (last and g == NG - 1):
                        place_max(NG * b + g + 2, (g + 1) % NG)
                    if not last:
                        sp.wait_ge(out_done, ST * (NG * b + g + 1))
                        load(b + 1, g)
                    sp.wait_ge(out_ready, NG * b + g + 1)
                    rows = attn_rows[b].rearrange("l d -> (l d)").rearrange(
                        "(h p x) -> p h x", h=H, p=P)[:, g * GH:(g + 1) * GH, :]
                    sp.dma_start(rows, attn_out[:, g % 2].rearrange("p j t e -> p j (t e)")).then_inc(attn_stored[g % 2], 16)

            batch(0, False)
            with sp.Fori(1, B - 1) as b:
                batch(b, False)
            batch(B - 1, True)
            for i in range(2):
                sp.wait_ge(attn_stored[i], 16 * NG // 2 * B)

        @block.scalar
        def _(act):
            def copy_max(count):
                act.wait_ge(max_turned, count)
                wait(act, max_placed, 32 * (count - 1))
                nc.scalar.activation(max_rows[:], psum[0:2 * GH, TURN, :], ACT.Copy).then_inc(max_copied, 1)

            def copy_out(count):
                act.wait_ge(out_done, ST * count)
                wait(act, out_turned, count - 1)
                nc.scalar.activation(o_raw[:], psum[:, OUTB, :], ACT.Copy).then_inc(out_copied, 1)

            def batch(b, last):
                for g in range(NG):
                    for st in range(ST):
                        step = ST * (NG * b + g) + st
                        for i in range(2):
                            act.wait_ge(keyed_done, 2 * step + i + 1)
                            if i == 0:
                                wait(act, out_done, step - 1 if (g or st > 1) else ST * NG * b)
                            nc.scalar.activation(
                                probs[:, st % 2, 2 * i:2 * i + 2, :], psum[:, KEYED + 2 * i:KEYED + 2 * i + 2, :],
                                ACT.Exp, scale=SCALE).then_inc(exp_done, 1)
                        if st == 0 and g > 0:
                            copy_out(NG * b + g)
                        if st == 5 and not (last and g == NG - 1):
                            copy_max(NG * b + g + 2)
                copy_out(NG * (b + 1))

            copy_max(1)
            batch(0, False)
            with act.Fori(1, B - 1) as b:
                batch(b, False)
            batch(B - 1, True)

        @block.vector
        def _(dve):
            def reduce(count, group, i):
                dve.wait_ge(scores_done, count + 1)
                nc.vector.tensor_reduce(max_part[:, group % 2, i // 8, i // 2 % GH, i % 2:i % 2 + 1],
                                        psum[:, MAXB + i % 2, :], AX_X, ALU.max).then_inc(scores_read, 1)

            def split_max(count, group):
                dve.wait_ge(scores_read, ITEMS * count)
                nc.vector.tensor_reduce(neg_max[:], max_part[:, group % 2], AX_X, ALU.max,
                                        negate=True).then_inc(max_ready, 1)
                dve.wait_ge(max_ready, count)
                wait(dve, max_turned, count - 1)
                nc.vector.tensor_copy(max_split[:, :, HI, :], neg_max[:]).then_inc(hi_ready, 1)
                dve.wait_ge(hi_ready, count)
                nc.vector.tensor_tensor(max_split[:, :, LO, :], neg_max[:], max_split[:, :, HI, :].bitcast(F32),
                                        ALU.subtract).then_inc(split_ready, 1)

            def normalise(count, b, g):
                dve.wait_ge(out_turned, count)
                turned = psum[:, TURN, :].rearrange("p (t j e) -> p t j e", t=LT, j=GH)
                nc.vector.reciprocal(recip[:], turned[:, :, :, E]).then_inc(recip_ready, 1)
                dve.wait_ge(recip_ready, count)
                wait(dve, attn_stored[g % 2], 16 * (NG // 2 * b + g // 2))
                dst = attn_out[:, g % 2].rearrange("p j t e -> p t j e")
                nc.vector.tensor_tensor(dst, turned[:, :, :, 0:E],
                                        recip[:].unsqueeze(3).to_broadcast([P, LT, GH, E]), ALU.mult).then_inc(out_ready, 1)

            for i in range(ITEMS):
                reduce(i, 0, i)
            split_max(1, 0)
            for i in range(ITEMS // 2):
                reduce(ITEMS + i, 1, i)

            def batch(b, last):
                for g in range(NG):
                    for st in range(ST):
                        ahead = 1 if st < ST // 2 else 2
                        if not (last and g + ahead >= NG):
                            for i in range(4):
                                item = (st * 4 + 16 + i) % ITEMS
                                reduce(ITEMS * (NG * b + g + ahead) + item, g + ahead, item)
                        if st == 1 and g > 0:
                            normalise(NG * b + g, b, g - 1)
                        if st == 3 and not (last and g == NG - 1):
                            split_max(NG * b + g + 2, g + 1)
                normalise(NG * (b + 1), b, NG - 1)

            batch(0, False)
            with dve.Fori(1, B - 1) as b:
                batch(b, False)
            batch(B - 1, True)

        @block.tensor
        def _(pe):
            def scores(count, g, i):
                t, j, half = i // 8, i // 2 % GH, i % 2
                wait(pe, scores_read, count - 1)
                nc.tensor.matmul(psum[:, MAXB + half, :], q_stack[:, g, j, t * P:(t + 1) * P],
                                 k_stack[:, g, j, half * 512:(half + 1) * 512], start=True,
                                 stop=True).then_inc(scores_done, 1)

            def turn_max(count):
                pe.wait_ge(split_ready, count)
                wait(pe, out_ready, count - 2)
                for t in range(LT):
                    last = nc.tensor.transpose(psum[0:2 * GH, TURN, t * P:(t + 1) * P],
                                               max_split[:, t].rearrange("p a j -> p (a j)").bitcast(F32), ident[:])
                last.then_inc(max_turned, 1)

            def turn_out(count, maxima):
                pe.wait_ge(out_copied, count)
                pe.wait_ge(max_copied, maxima)
                wait(pe, out_ready, count - 1)
                queries = o_raw[:].rearrange("c (p t) -> c p t", t=LT)
                for t in range(LT):
                    last = nc.tensor.transpose(psum[:, TURN, t * P:(t + 1) * P], queries[:, :, t], ident[:])
                last.then_inc(out_turned, 1)

            def keyed(step, g, st):
                for i in range(2):
                    wait(pe, exp_done, 2 * step + i - 1 if g or st else 2 * step)
                    for j in (2 * i, 2 * i + 1):
                        last = nc.tensor.matmul(psum[:, KEYED + j, :], k_stack[:, g, j, st * P:(st + 1) * P],
                                                q_stack[:, g, j, :], start=True, stop=True)
                    last.then_inc(keyed_done, 1)

            def weigh(step, g, st):
                pe.wait_ge(exp_done, 2 * (step + 1))
                for j in range(GH):
                    last = nc.tensor.matmul(psum[32 * j:32 * j + VW, OUTB, :], v_stack[:, g, st, j * VW:(j + 1) * VW],
                                            probs[:, st % 2, j, :], start=(st == 0), stop=(st == ST - 1),
                                            skip_group_check=True)
                last.then_inc(out_done, 1)

            pe.wait_ge(ones_set, 16 * SLOTS)
            pe.wait_ge(stack_loaded[0], 16 * LOADS)
            nc.tensor.matmul(psum[:, OUTB, :], q_stack[:, 0, 0, 0:P], q_stack[:, 0, 0, :], start=True, stop=True)
            for i in range(ITEMS):
                scores(i, 0, i)
            pe.wait_ge(stack_loaded[1], 16 * LOADS)
            turn_max(1)
            for i in range(ITEMS // 2):
                scores(ITEMS + i, 1, i)

            def batch(b, last):
                for g in range(NG):
                    for st in range(ST):
                        step = ST * (NG * b + g) + st
                        if st == 0:
                            pe.wait_ge(max_placed, 32 * (NG * b + g + 1))
                        keyed(step, g, st)
                        if g or st:
                            if st == 1 and g:
                                pe.wait_ge(out_copied, NG * b + g)
                            if st == 1 and not g:
                                wait(pe, out_copied, NG * b)
                            weigh(step - 1, (g if st else g - 1), (st - 1) % ST)
                        if st == 1 and g > 0:
                            turn_out(NG * b + g, NG * b + g + 1)
                        if st == 5 and not (last and g == NG - 1):
                            turn_max(NG * b + g + 2)
                        ahead = 1 if st < ST // 2 else 2
                        if not (last and g + ahead >= NG):
                            if st == ST // 2:
                                pe.wait_ge(stack_loaded[(g + 2) % NG], 16 * LOADS * (b + 1 + (g + 2) // NG))
                            for i in range(4):
                                item = (st * 4 + 16 + i) % ITEMS
                                scores(ITEMS * (NG * b + g + ahead) + item, (g + ahead) % NG, item)
                weigh(ST * NG * (b + 1) - 1, NG - 1, ST - 1)
                turn_out(NG * (b + 1), NG * (b + 1) + (0 if last else 1))

            batch(0, False)
            with pe.Fori(1, B - 1) as b:
                batch(b, False)
            batch(B - 1, True)


def feed_forward(nc, psum, ident, wo_t, wg1_t, attn_rows, w_raw, raw_loaded, x, bo, bg1, wg2, bg2, we, be, out):
    TOP = 8
    TERMS = [(HI, HI, k) for k in range(KC)] + [(LO, HI, k) for k in range(KC)] + [(HI, LO, k) for k in range(KC)]
    with ExitStack() as ctx:
        def sb(name, shape, dt):
            return ctx.enter_context(nc.sbuf_tensor(name, shape, dt))

        def sem(name):
            return ctx.enter_context(nc.semaphore(name))

        w_t = sb("w_t", [P, 2, KC, NX, D], F32R)
        total = sb("total", [P, NT, D], F32)
        x_bias = sb("x_bias", [P, 2, LT, D], F32)
        attn = sb("attn", [P, 2, LT, D], F32)
        attn_t = sb("attn_t", [P, 2, KC, L], F32R)
        x2_norm = sb("x2_norm", [P, LT, D], F32)
        x2_t = sb("x2_t", [P, 2, KC, NT * P], F32R)
        hidden = sb("hidden", [HID, 2, L], F32)
        bo_row = sb("bo_row", [P, D], F32)
        bg1_col = sb("bg1_col", [HID, 1], F32)
        wg2_sb = sb("wg2_sb", [HID, NX], F32)
        bg2_row = sb("bg2_row", [P, NX], F32)
        be_sb = sb("be_sb", [NX, D], F32)
        stats2 = sb("stats2", [P, LT, 6], F32)
        moments2 = sb("moments2", [P, LT, 2], F32)
        var2 = sb("var2", [P, LT], F32)
        minus_half2 = sb("minus_half2", [P, LT], F32)
        rstd2 = sb("rstd2", [P, LT], F32)
        iota_x = sb("iota_x", [P, NX], F32)
        logits = sb("logits", [P, NT, NX], F32)
        shifted = sb("shifted", [P, NT, NX], F32)
        neg_top = sb("neg_top", [P, NT], F32)
        exps = sb("exps", [P, NT, NX], F32)
        exp_sum = sb("exp_sum", [P, NT], F32)
        sum_inv = sb("sum_inv", [P, NT], F32)
        probs = sb("route_probs", [P, NT, NX], F32)
        top = sb("top", [P, NT, TOP], F32)
        top_at = sb("top_at", [P, NT, TOP], U32)
        top_at_f = sb("top_at_f", [P, NT, 2], F32)
        picked = sb("picked", [P, 2, NT, NX], F32)
        gates = sb("gates", [P, NT, NX], F32)
        gates_t = x_bias[0:NX].rearrange("x c t d -> x (c t d)")

        small_loaded = sem("small_loaded")
        consts_ready = sem("consts_ready")
        x_loaded = [sem(f"x2_loaded{i}") for i in range(2)]
        attn_loaded = [sem(f"attn_loaded{i}") for i in range(2)]
        bias_added = sem("bias_added")
        w_hi = sem("w_hi")
        w_lo = sem("w_lo")
        at_done = sem("at_done")
        at_hi = sem("at_hi")
        at_lo = sem("at_lo")
        proj_done = sem("oproj_done")
        total_ready = sem("total_ready")
        stats_done = sem("stats2_done")
        moments_done = sem("moments2_done")
        eps_added = sem("eps2_added")
        rstd_ready = sem("rstd2_ready")
        norm_ready = sem("norm2_ready")
        x2_done = sem("x2_done")
        x2_hi = sem("x2_hi")
        x2_lo = sem("x2_lo")
        hidden_done = sem("hidden_done")
        hidden_ready = sem("hidden_ready")
        logits_done = sem("logits_done")
        logits_ready = sem("logits_ready")
        neg_top_ready = sem("neg_top_ready")
        shifted_ready = sem("shifted_ready")
        exps_ready = sem("exps_ready")
        sum_ready = sem("sum_ready")
        inv_ready = sem("inv_ready")
        probs_ready = sem("probs_ready")
        top_ready = sem("top_ready")
        at_ready = sem("at_ready")
        at_f_ready = sem("at_f_ready")
        picked_ready = sem("picked_ready")
        gates_ready = sem("gates_ready")
        gates_turned = sem("gates_turned")
        gates_copied = sem("gates_copied")
        bias_done = sem("bias_done")
        bias_in = sem("bias_in")
        expert_done = sem("expert_done")
        expert_in = sem("expert_in")
        out_stored = sem("out_stored")

        SMALL = 5
        block = ctx.enter_context(nc.Block())

        @block.sync
        def _(sp):
            def load_attn(c):
                sp.dma_start(attn[:, c % 2], attn_rows[c].rearrange("(t p) d -> p t d", p=P)).then_inc(
                    attn_loaded[c % 2], 16)

            load_attn(0)
            sp.dma_start(bo_row[:], bo.partition_broadcast(P)).then_inc(small_loaded, 16)
            load_attn(1)
            for c in range(2):
                sp.dma_start(x_bias[:, c], x[c].rearrange("(t p) d -> p t d", p=P)).then_inc(x_loaded[c], 16)
            sp.dma_start(bg1_col[:], bg1.rearrange("(h o) -> h o", o=1), allow_slow_non_contiguous=True).then_inc(small_loaded, 16)
            sp.dma_start(wg2_sb[:], wg2[:, 0:NX]).then_inc(small_loaded, 16)
            sp.dma_start(bg2_row[:], bg2[0:NX].partition_broadcast(P)).then_inc(small_loaded, 16)
            sp.dma_start(be_sb[:], be).then_inc(small_loaded, 16)
            for p in range(RAW, PAIRS):
                sp.wait_ge(w_hi, p - RAW + 1)
                sp.wait_ge(w_lo, p - RAW + 1)
                load_pair(sp, we, w_raw, raw_loaded, p)
                if p in (RAW, RAW + 2):
                    c = 2 + (p - RAW) // 2
                    sp.wait_ge(at_done, KC * (c - 1))
                    load_attn(c)
                if p in (RAW + 1, RAW + 3):
                    c = 2 + (p - RAW - 1) // 2
                    sp.wait_ge(total_ready, 2 * (c - 1))
                    sp.dma_start(x_bias[:, c % 2], x[c].rearrange("(t p) d -> p t d", p=P)).then_inc(x_loaded[c % 2], 16)
            for c in range(B):
                sp.wait_ge(expert_in, 2 * NT * (PAIRS - 1) + 2 * LT * (c + 1))
                sp.dma_start(out[c].rearrange("(t p) d -> p t d", p=P),
                             total[:, LT * c:LT * (c + 1), :]).then_inc(out_stored, 16)
            sp.wait_ge(out_stored, 16 * B)

        @block.gpsimd
        def _(pool):
            nc.gpsimd.memset(minus_half2[:], -0.5).then_inc(consts_ready, 1)
            nc.gpsimd.iota(iota_x[:], pattern=[[1, NX]], base=0, channel_multiplier=0,
                           allow_small_or_imprecise_dtypes=True).then_inc(consts_ready, 1)
            pool.wait_ge(consts_ready, 1)
            pool.wait_ge(small_loaded, 16 * SMALL)

            def add_bias(c):
                pool.wait_ge(x_loaded[c % 2], 16 * (c // 2 + 1))
                nc.gpsimd.tensor_tensor(x_bias[:, c % 2], x_bias[:, c % 2],
                                        bo_row[:].unsqueeze(1).to_broadcast([P, LT, D]), ALU.add).then_inc(bias_added, 1)

            def split_weights(p):
                pool.wait_ge(w_hi, p + 1)
                nc.gpsimd.tensor_tensor(w_t[:, LO, :, 2 * p:2 * p + 2, :], w_raw[:, p % RAW],
                                        w_t[:, HI, :, 2 * p:2 * p + 2, :].bitcast(F32), ALU.subtract).then_inc(w_lo, 1)

            add_bias(0)
            add_bias(1)
            for c in range(B):
                split_weights(2 * c)
                if 1 <= c < B - 1:
                    add_bias(c + 1)
                pool.wait_ge(eps_added, c + 1)
                nc.gpsimd.tensor_tensor(rstd2[:], var2[:], minus_half2[:], ALU.pow).then_inc(rstd_ready, 1)
                split_weights(2 * c + 1)
            for p in range(2 * B, PAIRS):
                split_weights(p)

        @block.scalar
        def _(act):
            def round_weights(p):
                act.wait_ge(raw_loaded[p % RAW], 32 * (p // RAW + 1))
                nc.scalar.activation(w_t[:, HI, :, 2 * p:2 * p + 2, :], w_raw[:, p % RAW], ACT.Copy).then_inc(w_hi, 1)

            act.wait_ge(small_loaded, 16 * SMALL)
            round_weights(0)
            for c in range(B + 1):
                if c < B:
                    for k in range(KC):
                        act.wait_ge(at_done, KC * c + k + 1)
                        act.wait_ge(proj_done, 2 * c)
                        nc.scalar.activation(attn_t[:, HI, k, :], psum[:, k, :], ACT.Copy).then_inc(at_hi, 1)
                if c > 0:
                    for k in range(KC):
                        act.wait_ge(x2_done, KC * (c - 1) + k + 1)
                        nc.scalar.activation(x2_t[:, HI, k, (c - 1) * L:c * L], psum[:, 4 + k, :],
                                             ACT.Copy).then_inc(x2_hi, 1)
                    act.wait_ge(hidden_done, c)
                    nc.scalar.activation(hidden[:, (c - 1) % 2, :], psum[0:HID, 6, :], ACT.Gelu,
                                         bias=bg1_col[:]).then_inc(hidden_ready, 1)
                for p in range(2 * c + 1, min(2 * c + 3, PAIRS)):
                    round_weights(p)
            act.wait_ge(shifted_ready, 1)
            nc.scalar.activation(exps[:], shifted[:], ACT.Exp).then_inc(exps_ready, 1)
            for c in range(B):
                act.wait_ge(gates_turned, c + 1)
                nc.scalar.activation(gates_t[:, c * L:(c + 1) * L], psum[0:NX, c, :], ACT.Copy).then_inc(gates_copied, 1)

        @block.vector
        def _(dve):
            def residual(c):
                dve.wait_ge(bias_added, c + 1)
                for h in range(2):
                    dve.wait_ge(proj_done, 2 * c + h + 1)
                    t = LT * c + 2 * h
                    nc.vector.tensor_tensor(total[:, t:t + 2, :],
                                            psum[:, 2 + h, :].rearrange("p (t d) -> p t d", t=2),
                                            x_bias[:, c % 2, 2 * h:2 * h + 2, :], ALU.add).then_inc(total_ready, 1)

            def norm(c):
                for t in range(LT):
                    dve.wait_ge(total_ready, 2 * c + t // 2 + 1)
                    nc.vector.bn_stats(stats2[:, t, :], total[:, LT * c + t, :]).then_inc(stats_done, 1)
                for t in range(LT):
                    dve.wait_ge(stats_done, LT * c + t + 1)
                    nc.vector.bn_aggr(moments2[:, t, :], stats2[:, t, :]).then_inc(moments_done, 1)
                dve.wait_ge(moments_done, LT * (c + 1))
                nc.vector.tensor_scalar(var2[:], moments2[:, :, 1], EPS, None, ALU.add).then_inc(eps_added, 1)
                dve.wait_ge(rstd_ready, c + 1)
                if c > 0:
                    dve.wait_ge(x2_done, KC * c)
                for t in range(LT):
                    nc.vector.tensor_scalar(x2_norm[:, t, :], total[:, LT * c + t, :], moments2[:, t, 0:1],
                                            rstd2[:, t:t + 1], ALU.subtract, ALU.mult).then_inc(norm_ready, 1)

            for c in range(B + 1):
                if c < B:
                    for k in range(KC):
                        dve.wait_ge(at_hi, KC * c + k + 1)
                        nc.vector.tensor_tensor(attn_t[:, LO, k, :], psum[:, k, :], attn_t[:, HI, k, :].bitcast(F32),
                                                ALU.subtract).then_inc(at_lo, 1)
                if c > 0:
                    for k in range(KC):
                        dve.wait_ge(x2_hi, KC * (c - 1) + k + 1)
                        nc.vector.tensor_tensor(
                            x2_t[:, LO, k, (c - 1) * L:c * L], psum[:, 4 + k, :],
                            x2_t[:, HI, k, (c - 1) * L:c * L].bitcast(F32), ALU.subtract).then_inc(x2_lo, 1)
                if c < B:
                    residual(c)
                    norm(c)

            dve.wait_ge(logits_done, B)
            nc.vector.tensor_tensor(logits[:], psum[:, 7, 0:NT * NX].rearrange("p (t x) -> p t x", t=NT),
                                    bg2_row[:].unsqueeze(1).to_broadcast([P, NT, NX]), ALU.add).then_inc(logits_ready, 1)
            dve.wait_ge(logits_ready, 1)
            nc.vector.tensor_reduce(neg_top[:], logits[:], AX_X, ALU.max, negate=True).then_inc(neg_top_ready, 1)
            dve.wait_ge(neg_top_ready, 1)
            nc.vector.tensor_tensor(shifted[:], logits[:], neg_top[:].unsqueeze(2).to_broadcast([P, NT, NX]),
                                    ALU.add).then_inc(shifted_ready, 1)
            dve.wait_ge(exps_ready, 1)
            nc.vector.tensor_reduce(exp_sum[:], exps[:], AX_X, ALU.add).then_inc(sum_ready, 1)
            dve.wait_ge(sum_ready, 1)
            nc.vector.reciprocal(sum_inv[:], exp_sum[:]).then_inc(inv_ready, 1)
            dve.wait_ge(inv_ready, 1)
            nc.vector.tensor_tensor(probs[:], exps[:], sum_inv[:].unsqueeze(2).to_broadcast([P, NT, NX]),
                                    ALU.mult).then_inc(probs_ready, 1)
            dve.wait_ge(probs_ready, 1)
            for t in range(NT):
                nc.vector.max(top[:, t, :], probs[:, t, :]).then_inc(top_ready, 1)
            for t in range(NT):
                dve.wait_ge(top_ready, t + 1)
                nc.vector.max_index(top_at[:, t, :], top[:, t, :], probs[:, t, :]).then_inc(at_ready, 1)
            dve.wait_ge(at_ready, NT)
            nc.vector.tensor_copy(top_at_f[:], top_at[:, :, 0:2]).then_inc(at_f_ready, 1)
            dve.wait_ge(at_f_ready, 1)
            for i in range(2):
                for t in range(NT):
                    nc.vector.tensor_scalar(picked[:, i, t, :], iota_x[:], top_at_f[:, t, i:i + 1], top[:, t, i:i + 1],
                                            ALU.is_equal, ALU.mult).then_inc(picked_ready, 1)
            dve.wait_ge(picked_ready, 2 * NT)
            nc.vector.tensor_tensor(gates[:], picked[:, 0], picked[:, 1], ALU.add).then_inc(gates_ready, 1)
            dve.wait_ge(gates_ready, 1)

            def experts(p):
                dve.wait_ge(expert_in, 2 * NT * p)
                for t in range(0, NT, 2):
                    for e in range(2):
                        for u in (t, t + 1):
                            if e == 0:
                                dve.wait_ge(expert_done, NT * p + u + 1)
                            else:
                                dve.wait_ge(expert_in, 2 * NT * p + 2 * t + (u - t) + 1)
                            nc.vector.scalar_tensor_tensor(
                                out=total[:, u, :], in0=psum[:, u % 8, e * D:(e + 1) * D],
                                scalar=gates[:, u, bass.ds(2 * p + e, 1)], in1=total[:, u, :],
                                op0=ALU.mult, op1=ALU.add).then_inc(expert_in, 1)

            experts(0)
            dve.wait_ge(expert_in, 2 * NT)
            for n in range(NT // 2):
                dve.wait_ge(bias_done, n + 1)
                nc.vector.tensor_tensor(total[:, 2 * n:2 * n + 2, :], total[:, 2 * n:2 * n + 2, :],
                                        psum[:, n, :].rearrange("p (t d) -> p t d", t=2), ALU.add).then_inc(bias_in, 1)
            dve.wait_ge(bias_in, NT // 2)
            with dve.Fori(1, PAIRS) as p:
                experts(p)

        @block.tensor
        def _(pe):
            pe.wait_ge(small_loaded, 16 * SMALL)
            for c in range(B + 2):
                if c < B:
                    pe.wait_ge(attn_loaded[c % 2], 16 * (c // 2 + 1))
                    if c > 0:
                        pe.wait_ge(at_lo, KC * c)
                    for k in range(KC):
                        for t in range(LT):
                            last = nc.tensor.transpose(psum[:, k, t * P:(t + 1) * P],
                                                       attn[:, c % 2, t, k * P:(k + 1) * P], ident[:])
                        last.then_inc(at_done, 1)
                if 1 <= c <= B:
                    pe.wait_ge(norm_ready, LT * c)
                    if c > 1:
                        pe.wait_ge(x2_lo, KC * (c - 1))
                    for k in range(KC):
                        for t in range(LT):
                            last = nc.tensor.transpose(psum[:, 4 + k, t * P:(t + 1) * P],
                                                       x2_norm[:, t, k * P:(k + 1) * P], ident[:])
                        last.then_inc(x2_done, 1)
                if c < B:
                    pe.wait_ge(at_lo, KC * (c + 1))
                    for h in range(2):
                        if c > 0:
                            pe.wait_ge(total_ready, 2 * (c - 1) + h + 1)
                        for u in range(2):
                            t = 2 * h + u
                            for m, (a, w, k) in enumerate(TERMS):
                                last = nc.tensor.matmul(psum[:, 2 + h, u * D:(u + 1) * D],
                                                        attn_t[:, a, k, t * P:(t + 1) * P], wo_t[:, w, k, :],
                                                        start=(m == 0), stop=(m == len(TERMS) - 1))
                        last.then_inc(proj_done, 1)
                if 1 <= c <= B:
                    pe.wait_ge(x2_lo, KC * c)
                    if c > 1:
                        pe.wait_ge(hidden_ready, c - 1)
                    for m, (a, w, k) in enumerate(TERMS):
                        last = nc.tensor.matmul(psum[:, 6, :], wg1_t[:, w, k, :], x2_t[:, a, k, (c - 1) * L:c * L],
                                                start=(m == 0), stop=(m == len(TERMS) - 1))
                    last.then_inc(hidden_done, 1)
                if c >= 2:
                    pe.wait_ge(hidden_ready, c - 1)
                    for t in range(LT):
                        n = LT * (c - 2) + t
                        last = nc.tensor.matmul(psum[:, 7, n * NX:(n + 1) * NX], hidden[:, c % 2, t * P:(t + 1) * P],
                                                wg2_sb[:], start=True, stop=True)
                    last.then_inc(logits_done, 1)

            def experts(p, first):
                if first:
                    pe.wait_ge(w_lo, 1)
                else:
                    pe.wait_ge(w_lo, p + 1)
                for t in range(NT):
                    if not first:
                        pe.wait_ge(expert_in, 2 * NT * p + 4 * ((t - 8) // 2 + 1))
                    elif t >= 8:
                        pe.wait_ge(expert_in, 4 * ((t - 8) // 2 + 1))
                    elif t == 7:
                        pe.wait_ge(logits_ready, 1)
                    for m, (a, w, k) in enumerate(TERMS):
                        last = nc.tensor.matmul(psum[:, t % 8, :], x2_t[:, a, k, t * P:(t + 1) * P],
                                                w_t[:, w, k, bass.ds(2 * p, 2), :], start=(m == 0),
                                                stop=(m == len(TERMS) - 1))
                    last.then_inc(expert_done, 1)

            experts(0, True)
            pe.wait_ge(gates_ready, 1)
            pe.wait_ge(expert_in, 2 * NT)
            for c in range(B):
                for t in range(LT):
                    last = nc.tensor.transpose(psum[0:NX, c, t * P:(t + 1) * P], gates[:, LT * c + t, :], ident[:])
                last.then_inc(gates_turned, 1)
            pe.wait_ge(gates_copied, B)
            for n in range(NT // 2):
                for t in (2 * n, 2 * n + 1):
                    last = nc.tensor.matmul(psum[:, n, (t % 2) * D:(t % 2 + 1) * D], gates_t[:, t * P:(t + 1) * P],
                                            be_sb[:], start=True, stop=True)
                last.then_inc(bias_done, 1)
            pe.wait_ge(bias_in, NT // 2)
            with pe.Fori(1, PAIRS) as p:
                experts(p, False)


_INS = ['x', 'ctx_1024', 'L0_xattn_Wq', 'L0_xattn_bq', 'L0_xattn_Wo', 'L0_xattn_bo', 'L0_ffn_wg1', 'L0_ffn_bg1',
        'L0_ffn_wg2', 'L0_ffn_bg2', 'L0_ffn_We', 'L0_ffn_be']
_OUT = ((B, L, D), 'float32')


def kernel(**inputs):
    import numpy as _np
    import concourse.bacc as _bacc
    from concourse import mybir as _mybir
    from concourse.bass_utils import run_bass_kernel_spmd as _run

    nc = _bacc.Bacc("TRN2", target_bir_lowering=False, num_devices=1)
    arrays, args = {}, []
    for name in _INS:
        a = _np.ascontiguousarray(inputs[name])
        arrays[f"in_{name}_dram"] = a
        args.append(nc.dram_tensor(f"in_{name}_dram", a.shape, _mybir.dt.from_np(a.dtype), kind="ExternalInput").ap())
    args.append(nc.dram_tensor("out_dram", _OUT[0], _mybir.dt.from_np(_np.dtype(_OUT[1])), kind="ExternalOutput").ap())
    mixed_kernel(nc, *args)
    r = _run(nc, [arrays], core_ids=[0])
    return r.results[0]["out_dram"]
```

```python
from contextlib import ExitStack

import concourse.bass as bass
from concourse import mybir

ALU = mybir.AluOpType
ACT = mybir.ActivationFunctionType
AX_X = mybir.AxisListType.X
F32 = mybir.dt.float32
F32R = mybir.dt.float32r
U32 = mybir.dt.uint32

P = 128
B, L, S, D = 4, 512, 1024, 256
H = 16
E = D // H
KC = D // P
NX = 20
HID = D // 4
GH = 4
NG = H // GH
LT = L // P
ST = S // P
NT = B * LT
SCALE = float(E) ** -0.5
EPS = 1e-5
VW = E + 1
PAIRS = NX // 2
LOADS = 8
RAW = 3

Q_SLABS = (0, 0, 1)
K_SLABS = (0, 1, 0)
MROW = 3 * E
HI, LO = 0, 1
TERMS = [(a, w, k) for a, w in ((HI, HI), (LO, HI), (HI, LO)) for k in range(KC)]


def wait(eng, sem, value):
    if not isinstance(value, int) or value > 0:
        eng.wait_ge(sem, value)


def mixed_kernel(nc, x, ctx_in, wq, bq, wo, bo, wg1, bg1, wg2, bg2, we, be, out):
    q_parts = nc.dram_tensor("q_parts", [B, 2, NG, GH, E, L], F32, kind="Internal").ap()
    k_parts = nc.dram_tensor("k_parts", [B, 2, NG, GH, E, S], F32, kind="Internal").ap()
    attn_rows = nc.dram_tensor("attn_rows", [B, L, D], F32, kind="Internal").ap()
    v_parts = nc.dram_tensor("v_parts", [B, NG, P, ST, GH * VW], F32, kind="Internal").ap()

    with ExitStack() as whole:
        def kept(name, shape, dt):
            return whole.enter_context(nc.sbuf_tensor(name, shape, dt))

        psum = whole.enter_context(nc.psum_tensor("psum", [P, 8, 512], F32))
        ident = kept("ident", [P, P], F32)
        wo_t = kept("wo_t", [P, 2, KC, D], F32R)
        wg1_t = kept("wg1_t", [P, 2, KC, P], F32R)
        w_raw = kept("w_raw", [P, RAW, KC, 2, D], F32)
        raw_loaded = [whole.enter_context(nc.semaphore(f"raw_loaded{i}")) for i in range(RAW)]
        with ExitStack() as early:
            q_stack = early.enter_context(nc.sbuf_tensor("q_stack", [P, NG, GH, L], F32R))
            k_stack = early.enter_context(nc.sbuf_tensor("k_stack", [P, NG, GH, S], F32R))
            v_stack = early.enter_context(nc.sbuf_tensor("v_stack", [P, NG, ST, GH * VW], F32))
            zero_rows = early.enter_context(nc.sbuf_tensor("zero_rows", [2, L], F32))
            stack_loaded = [early.enter_context(nc.semaphore(f"stack_loaded{g}")) for g in range(NG)]

            def load_stack(sp, b, g):
                for r, part in enumerate(Q_SLABS):
                    sp.dma_start(q_stack[r * E:(r + 1) * E, g, :, :].bitcast(F32),
                                 q_parts[b, part, g].rearrange("j e l -> e j l")).then_inc(stack_loaded[g], 16)
                for r, part in enumerate(K_SLABS):
                    sp.dma_start(k_stack[r * E:(r + 1) * E, g, :, :].bitcast(F32),
                                 k_parts[b, part, g].rearrange("j e s -> e j s")).then_inc(stack_loaded[g], 16)
                sp.dma_start(q_stack[MROW:MROW + 2, g, :, :].bitcast(F32),
                             zero_rows[:].unsqueeze(1).to_broadcast([2, GH, L])).then_inc(stack_loaded[g], 16)
                sp.dma_start(v_stack[:, g, :, :], v_parts[b, g]).then_inc(stack_loaded[g], 16)

            project(nc, psum, ident, wo_t, wg1_t, q_stack, k_stack, zero_rows, load_stack,
                    x, ctx_in, wq, bq, wo, wg1, q_parts, k_parts, v_parts)
            attend(nc, psum, ident, q_stack, k_stack, v_stack, stack_loaded, load_stack, attn_rows, we, w_raw,
                   raw_loaded)
        feed_forward(nc, psum, ident, wo_t, wg1_t, attn_rows, w_raw, raw_loaded, x, bo, bg1, wg2, bg2, we, be, out)


def load_pair(sp, we, w_raw, raw_loaded, p):
    for i in range(2):
        sp.dma_start(w_raw[:, p % RAW, :, i, :], we[2 * p + i].rearrange("(k p) o -> p k o", p=P)).then_inc(
            raw_loaded[p % RAW], 16)


def project(nc, psum, ident, wo_t, wg1_t, q_stack, k_stack, zero_rows, load_stack,
            x, ctx_in, wq, bq, wo, wg1, q_parts, k_parts, v_parts):
    TILES = LT
    CH = S // L
    CHUNKS = CH + 1
    NTR = CHUNKS * KC
    TURNED = (0, 6, 0)
    PROJ, VALS = 2, 4
    with ExitStack() as ctx:
        def sb(name, shape, dt):
            return ctx.enter_context(nc.sbuf_tensor(name, shape, dt))

        def sem(name):
            return ctx.enter_context(nc.semaphore(name))

        w_nat = sb("w_nat", [P, 2, KC, D], F32)
        g_nat = sb("g_nat", [P, KC, P], F32)
        wq_t = sb("wq_t", [P, 2, KC, D], F32R)
        bq_col = sb("bq_col", [P, KC], F32)
        bq_row = sb("bq_row", [P, D], F32)
        x_in = sb("x_in", [P, TILES, D], F32)
        c_in = [sb(f"c_in{i}", [P, TILES, D], F32) for i in range(CH)]
        stats = sb("stats", [P, TILES, 6], F32)
        mean_gap = sb("mean_gap", [P, TILES], F32)
        squares = sb("squares", [P, TILES], F32)
        gap_square = sb("gap_square", [P, TILES], F32)
        mean = sb("mean", [P, TILES], F32)
        var = sb("var", [P, TILES], F32)
        var_eps = sb("var_eps", [P, TILES], F32)
        minus_half = sb("minus_half", [P, TILES], F32)
        rstd = sb("rstd", [P, TILES], F32)
        one_row = sb("one_row", [2, L], F32)
        tok_t = [sb(f"tok_t{n}", [P, 2, KC, L], F32R) for n in range(CHUNKS)]
        stage = [[sb(f"stage{n}{c}", [P, 2, L], F32R) for c in range(KC)] for n in range(CHUNKS)]
        v_stage = [sb(f"v_stage{i}", [P, NG, TILES, GH * VW], F32) for i in range(CH)]

        wq_loaded = sem("wq_loaded")
        consts_loaded = sem("consts_loaded")
        g_zeroed = sem("g_zeroed")
        g_loaded = sem("g_loaded")
        ident_zeroed = sem("ident_zeroed")
        ident_ready = sem("ident_ready")
        filled = sem("filled")
        cleared = sem("cleared")
        ones_set = sem("ones_set")
        wt_done = sem("wt_done")
        wt_hi = sem("wt_hi")
        wt_lo = sem("wt_lo")
        x_loaded = sem("x_loaded")
        c_loaded = [sem(f"c_loaded{i}") for i in range(CH)]
        stats_done = sem("stats_done")
        gap_done = sem("gap_done")
        squares_done = sem("squares_done")
        mean_ready = sem("mean_ready")
        square_done = sem("square_done")
        var_done = sem("var_done")
        eps_added = sem("eps_added")
        rstd_ready = sem("rstd_ready")
        norm_ready = sem("norm_ready")
        tok_done = sem("tok_done")
        tok_hi = sem("tok_hi")
        tok_lo = sem("tok_lo")
        proj_done = sem("proj_done")
        proj_hi = sem("proj_hi")
        proj_lo = sem("proj_lo")
        stored = [[sem(f"stored{n}{c}") for c in range(KC)] for n in range(CHUNKS)]
        v_done = sem("v_done")
        v_ready = sem("v_ready")
        v_stored = [sem(f"v_stored{i}") for i in range(CH)]

        block = ctx.enter_context(nc.Block())

        @block.sync
        def _(sp):
            sp.dma_start(w_nat[:, 0], wq.rearrange("(c p) i -> p c i", p=P)).then_inc(wq_loaded, 16)
            sp.dma_start(bq_col[:], bq.rearrange("(c p) -> p c", p=P),
                         allow_slow_non_contiguous=True).then_inc(consts_loaded, 16)
            sp.dma_start(bq_row[:], bq.partition_broadcast(P)).then_inc(consts_loaded, 16)
            sp.dma_start(w_nat[:, 1], wo.rearrange("(c p) i -> p c i", p=P)).then_inc(consts_loaded, 16)
            sp.wait_ge(g_zeroed, 1)
            sp.dma_start(g_nat[:, :, 0:HID], wg1.rearrange("(k p) h -> p k h", p=P)).then_inc(g_loaded, 16)

            def store_parts(b, n):
                for c in range(KC):
                    sp.wait_ge(proj_lo, NTR * b + KC * n + c + 1)
                    for part in range(2):
                        src = stage[n][c][:, part, :].bitcast(F32)
                        rows = slice(c * P, (c + 1) * P)
                        if n == CH:
                            dst = q_parts[b, part].rearrange("g j e l -> (g j e) l")[rows, :]
                        else:
                            dst = k_parts[b, part].rearrange("g j e l -> (g j e) l")[rows, n * L:(n + 1) * L]
                        sp.dma_start(dst, src).then_inc(stored[n][c], 16)

            def store_values(b, i):
                sp.wait_ge(v_ready, 2 * TILES * b + TILES * (i + 1))
                dst = v_parts[b, :, :, i * TILES:(i + 1) * TILES, :].rearrange("g p t v -> p g t v")
                sp.dma_start(dst, v_stage[i][:]).then_inc(v_stored[i], 16)

            def batch(b):
                for i in range(CH):
                    store_parts(b, i)
                    store_values(b, i)
                store_parts(b, CH)

            def all_stored(batches):
                for n in range(CHUNKS):
                    for c in range(KC):
                        sp.wait_ge(stored[n][c], 2 * 16 * batches)
                for i in range(CH):
                    sp.wait_ge(v_stored[i], 16 * batches)

            batch(0)
            sp.wait_ge(cleared, 4)
            sp.dma_start(k_stack[MROW:MROW + 2].rearrange("p g j s -> p (g j s)").rearrange(
                "p (n l) -> p n l", l=L).bitcast(F32), one_row[:].unsqueeze(1).to_broadcast([2, NG * GH * S // L, L])
            ).then_inc(ones_set, 16)
            all_stored(1)
            load_stack(sp, 0, 0)
            with sp.Fori(1, B - 1) as b:
                batch(b)
            batch(B - 1)
            sp.wait_ge(ones_set, 16)
            all_stored(B)

        @block.gpsimd
        def _(pool):
            nc.gpsimd.memset(ident[:], 0.0).then_inc(ident_zeroed, 1)
            nc.gpsimd.memset(g_nat[:], 0.0).then_inc(g_zeroed, 1)
            pool.wait_ge(ident_zeroed, 1)
            nc.gpsimd.affine_select(out=ident[:], in_=ident[:], compare_op=ALU.not_equal, fill=1.0, base=0,
                                    pattern=[[-1, P]], channel_multiplier=1).then_inc(ident_ready, 1)
            nc.gpsimd.memset(minus_half[:], -0.5).then_inc(filled, 1)
            for i in range(CH):
                nc.gpsimd.memset(v_stage[i][:], 1.0).then_inc(filled, 1)
            pool.wait_ge(filled, 1)

            def batch(b):
                pool.wait_ge(eps_added, b + 1)
                nc.gpsimd.tensor_tensor(rstd[:], var_eps[:], minus_half[:], ALU.pow).then_inc(rstd_ready, 1)

            nc.gpsimd.memset(zero_rows[:], 0.0).then_inc(cleared, 1)
            nc.gpsimd.memset(one_row[:], 1.0).then_inc(cleared, 1)
            nc.gpsimd.memset(q_stack[:].bitcast(F32), 0.0).then_inc(cleared, 1)
            batch(0)
            nc.gpsimd.memset(k_stack[:].bitcast(F32), 0.0).then_inc(cleared, 1)
            with pool.Fori(1, B) as b:
                batch(b)

        @block.vector
        def _(dve):
            def split_weights(n, dst):
                dve.wait_ge(wt_hi, n + 1)
                src = psum[:, 2 + n, :].rearrange("p (k o) -> p k o", k=KC)
                nc.vector.tensor_tensor(dst[:, LO], src, dst[:, HI].bitcast(F32), ALU.subtract).then_inc(wt_lo, 1)

            def split_tok(b, n):
                for k in range(KC):
                    dve.wait_ge(tok_hi, NTR * b + KC * n + k + 1)
                    nc.vector.tensor_tensor(tok_t[n][:, LO, k, :], psum[:, TURNED[n] + k, :],
                                            tok_t[n][:, HI, k, :].bitcast(F32), ALU.subtract).then_inc(tok_lo, 1)

            def split_proj(b, n):
                for c in range(KC):
                    dve.wait_ge(proj_hi, NTR * b + KC * n + c + 1)
                    nc.vector.scalar_tensor_tensor(
                        out=stage[n][c][:, LO, :], in0=psum[:, PROJ + c, :], scalar=bq_col[:, c:c + 1],
                        in1=stage[n][c][:, HI, :].bitcast(F32), op0=ALU.add, op1=ALU.subtract).then_inc(proj_lo, 1)

            def take_values(b, i):
                wait(dve, v_stored[i], 16 * b)
                for t in range(TILES):
                    dve.wait_ge(v_done, 2 * CH * b + 2 * i + t // 2 + 1)
                    dst = v_stage[i][:, :, t, :].rearrange("p g (j v) -> p g j v", j=GH)[:, :, :, 0:E]
                    src = psum[:, VALS + t // 2, (t % 2) * D:(t % 2 + 1) * D]
                    nc.vector.tensor_tensor(
                        dst, src.rearrange("p (g j e) -> p g j e", g=NG, j=GH),
                        bq_row[:].rearrange("p (g j e) -> p g j e", g=NG, j=GH), ALU.add).then_inc(v_ready, 1)

            def layer_norm(b):
                dve.wait_ge(x_loaded, 16 * (b + 1))
                for t in range(TILES):
                    nc.vector.bn_stats(stats[:, t, :], x_in[:, t, :]).then_inc(stats_done, 1)
                dve.wait_ge(stats_done, TILES * (b + 1))
                nc.vector.tensor_tensor(mean_gap[:], stats[:, :, 1], stats[:, :, 4], ALU.subtract).then_inc(gap_done, 1)
                nc.vector.tensor_tensor(squares[:], stats[:, :, 2], stats[:, :, 5], ALU.add).then_inc(squares_done, 1)
                dve.wait_ge(gap_done, b + 1)
                nc.vector.scalar_tensor_tensor(out=mean[:], in0=mean_gap[:], scalar=-0.5, in1=stats[:, :, 1],
                                               op0=ALU.mult, op1=ALU.add).then_inc(mean_ready, 1)
                nc.vector.scalar_tensor_tensor(out=gap_square[:], in0=mean_gap[:], scalar=0.25, in1=mean_gap[:],
                                               op0=ALU.mult, op1=ALU.mult).then_inc(square_done, 1)
                dve.wait_ge(squares_done, b + 1)
                dve.wait_ge(square_done, b + 1)
                nc.vector.scalar_tensor_tensor(out=var[:], in0=squares[:], scalar=1.0 / D, in1=gap_square[:],
                                               op0=ALU.mult, op1=ALU.add).then_inc(var_done, 1)
                dve.wait_ge(var_done, b + 1)
                nc.vector.tensor_scalar(var_eps[:], var[:], EPS, None, ALU.add).then_inc(eps_added, 1)
                dve.wait_ge(mean_ready, b + 1)
                dve.wait_ge(rstd_ready, b + 1)
                for t in range(TILES):
                    nc.vector.tensor_scalar(x_in[:, t, :], x_in[:, t, :], mean[:, t:t + 1], rstd[:, t:t + 1],
                                            ALU.subtract, ALU.mult).then_inc(norm_ready, 1)

            def batch(b, first):
                split_tok(b, 0)
                if not first:
                    split_proj(b - 1, 2)
                split_tok(b, 1)
                layer_norm(b)
                split_proj(b, 0)
                take_values(b, 0)
                split_tok(b, 2)
                split_proj(b, 1)
                take_values(b, 1)

            split_weights(0, wq_t)
            dve.wait_ge(consts_loaded, 48)
            dve.wait_ge(filled, CHUNKS)
            batch(0, True)
            with dve.Fori(1, B) as b:
                batch(b, False)
            split_proj(B - 1, 2)
            split_weights(1, wo_t)
            dve.wait_ge(wt_hi, 3)
            nc.vector.tensor_tensor(wg1_t[:, LO], g_nat[:], wg1_t[:, HI].bitcast(F32),
                                    ALU.subtract).then_inc(wt_lo, 1)

        @block.scalar
        def _(act):
            def load_tokens(b, n):
                src = x[b] if n == CH else ctx_in[b, n * L:(n + 1) * L, :]
                dst, done = (x_in, x_loaded) if n == CH else (c_in[n], c_loaded[n])
                act.dma_start(dst[:], src.rearrange("(t p) d -> p t d", p=P)).then_inc(done, 16)

            def round_weights(n, dst):
                act.wait_ge(wt_done, n + 1)
                src = psum[:, 2 + n, :].rearrange("p (k o) -> p k o", k=KC)
                nc.scalar.activation(dst[:, HI], src, ACT.Copy).then_inc(wt_hi, 1)

            def round_tok(b, n, last):
                for k in range(KC):
                    act.wait_ge(tok_done, NTR * b + KC * n + k + 1)
                    nc.scalar.activation(tok_t[n][:, HI, k, :], psum[:, TURNED[n] + k, :], ACT.Copy).then_inc(tok_hi, 1)
                if not last:
                    load_tokens(b + 1, n)

            def round_proj(b, n):
                for c in range(KC):
                    act.wait_ge(proj_done, NTR * b + KC * n + c + 1)
                    wait(act, stored[n][c], 2 * 16 * b)
                    nc.scalar.activation(stage[n][c][:, HI, :], psum[:, PROJ + c, :], ACT.Identity,
                                         bias=bq_col[:, c:c + 1]).then_inc(proj_hi, 1)

            def batch(b, first, last):
                round_tok(b, 0, last)
                if not first:
                    round_proj(b - 1, 2)
                round_tok(b, 1, last)
                round_proj(b, 0)
                round_tok(b, 2, last)
                round_proj(b, 1)

            for n in range(CHUNKS):
                load_tokens(0, n)
            round_weights(0, wq_t)
            act.wait_ge(consts_loaded, 48)
            batch(0, True, False)
            with act.Fori(1, B - 1) as b:
                batch(b, False, False)
            batch(B - 1, False, True)
            round_proj(B - 1, 2)
            round_weights(1, wo_t)
            act.wait_ge(g_loaded, 16)
            nc.scalar.activation(wg1_t[:, HI], g_nat[:], ACT.Copy).then_inc(wt_hi, 1)

        @block.tensor
        def _(pe):
            def turn_weights(n):
                for k in range(KC):
                    for c in range(KC):
                        last = nc.tensor.transpose(psum[:, 2 + n, k * D + c * P:k * D + (c + 1) * P],
                                                   w_nat[:, n, c, k * P:(k + 1) * P], ident[:])
                last.then_inc(wt_done, 1)

            def turn_tokens(b, n):
                if n == CH:
                    pe.wait_ge(norm_ready, TILES * (b + 1))
                    src = x_in
                    pe.wait_ge(tok_lo, NTR * b + KC)
                else:
                    pe.wait_ge(c_loaded[n], 16 * (b + 1))
                    src = c_in[n]
                    wait(pe, tok_lo, NTR * b)
                for k in range(KC):
                    for t in range(TILES):
                        last = nc.tensor.transpose(psum[:, TURNED[n] + k, t * P:(t + 1) * P],
                                                   src[:, t, k * P:(k + 1) * P], ident[:])
                    last.then_inc(tok_done, 1)

            def projections(b, n):
                pe.wait_ge(tok_lo, NTR * b + KC * (n + 1))
                for c in range(KC):
                    wait(pe, proj_lo, NTR * b + KC * n + c - 1)
                    for m, (a, w, k) in enumerate(TERMS):
                        last = nc.tensor.matmul(psum[:, PROJ + c, :], wq_t[:, w, k, c * P:(c + 1) * P],
                                                tok_t[n][:, a, k, :], start=(m == 0), stop=(m == len(TERMS) - 1))
                    last.then_inc(proj_done, 1)

            def values(b, i):
                for pr in range(2):
                    wait(pe, v_ready, TILES * (CH * b + i - 1) + 2 * (pr + 1))
                    for t in (2 * pr, 2 * pr + 1):
                        for m, (a, w, k) in enumerate(TERMS):
                            last = nc.tensor.matmul(psum[:, VALS + pr, (t % 2) * D:(t % 2 + 1) * D],
                                                    tok_t[i][:, a, k, t * P:(t + 1) * P], wq_t[:, w, k, :],
                                                    start=(m == 0), stop=(m == len(TERMS) - 1))
                    last.then_inc(v_done, 1)

            def batch(b, first):
                turn_tokens(b, 0)
                if not first:
                    projections(b - 1, 2)
                turn_tokens(b, 1)
                projections(b, 0)
                values(b, 0)
                turn_tokens(b, 2)
                projections(b, 1)
                values(b, 1)

            pe.wait_ge(ident_ready, 1)
            pe.wait_ge(wq_loaded, 16)
            turn_weights(0)
            pe.wait_ge(wt_lo, 1)
            batch(0, True)
            with pe.Fori(1, B) as b:
                batch(b, False)
            projections(B - 1, 2)
            pe.wait_ge(consts_loaded, 48)
            pe.wait_ge(proj_lo, NTR * B)
            turn_weights(1)


def attend(nc, psum, ident, q_stack, k_stack, v_stack, stack_loaded, load_stack, attn_rows, we, w_raw,
           raw_loaded):
    SLOTS = NG
    ITEMS = LT * GH * 2
    PB = 4
    LAG = 2
    with ExitStack() as ctx:
        def sb(name, shape, dt):
            return ctx.enter_context(nc.sbuf_tensor(name, shape, dt))

        def sem(name):
            return ctx.enter_context(nc.semaphore(name))

        probs = sb("probs", [P, PB, GH, L], F32)
        max_part = sb("max_part", [P, 2, LT, GH, 2], F32)
        neg_max = sb("neg_max", [P, LT, GH], F32)
        max_split = sb("max_split", [P, LT, 2, GH], F32R)
        max_rows = sb("max_rows", [2 * GH, L], F32)
        o_raw = sb("o_raw", [P, L], F32)
        recip = sb("recip", [P, LT, GH], F32)
        attn_out = sb("attn_out", [P, 2, GH, LT, E], F32)

        scores_done = sem("scores_done")
        scores_read = sem("scores_read")
        max_ready = sem("max_ready")
        hi_ready = sem("hi_ready")
        split_ready = sem("split_ready")
        max_turned = sem("max_turned")
        max_copied = sem("max_copied")
        max_placed = sem("max_placed")
        keyed_done = sem("keyed_done")
        exp_done = sem("exp_done")
        out_done = sem("out_done")
        out_copied = sem("out_copied")
        out_turned = sem("out_turned")
        recip_ready = sem("recip_ready")
        out_ready = sem("out_ready")
        attn_stored = [sem(f"attn_stored{i}") for i in range(2)]

        KEYED, MAXB, OUTB = 0, 4, 7
        TURN_OUT, TURN_MAX = LAG, 5
        EXTRAS = (0, TURN_OUT, TURN_MAX, ST - 1)
        FIRST = ITEMS * 3 // 2

        def slot(st, i):
            return MAXB + (4 * st + i + sum(e < st for e in EXTRAS)) % 3


        block = ctx.enter_context(nc.Block())

        @block.sync
        def _(sp):
            def place_max(count, g):
                sp.wait_ge(max_copied, count)
                for part in range(2):
                    sp.dma_start(q_stack[MROW + part:MROW + part + 1, g, :, :].bitcast(F32),
                                 max_rows[part * GH:(part + 1) * GH, :]).then_inc(max_placed, 16)

            for g in range(1, NG):
                load_stack(sp, 0, g)
            place_max(1, 0)
            for p in range(RAW):
                load_pair(sp, we, w_raw, raw_loaded, p)

            def batch(b, last):
                for g in range(NG):
                    if not (last and g == NG - 1):
                        place_max(NG * b + g + 2, (g + 1) % NG)
                    if not last:
                        sp.wait_ge(out_done, ST * (NG * b + g + 1))
                        load_stack(sp, b + 1, g)
                    sp.wait_ge(out_ready, NG * b + g + 1)
                    rows = attn_rows[b].rearrange("l d -> (l d)").rearrange(
                        "(h p x) -> p h x", h=H, p=P)[:, g * GH:(g + 1) * GH, :]
                    sp.dma_start(rows, attn_out[:, g % 2].rearrange("p j t e -> p j (t e)")).then_inc(attn_stored[g % 2], 16)

            batch(0, False)
            with sp.Fori(1, B - 1) as b:
                batch(b, False)
            batch(B - 1, True)
            for i in range(2):
                sp.wait_ge(attn_stored[i], 16 * NG // 2 * B)

        @block.scalar
        def _(act):
            def copy_max(count, bank):
                act.wait_ge(max_turned, count)
                wait(act, max_placed, 32 * (count - 1))
                nc.scalar.activation(max_rows[:], psum[0:2 * GH, bank, :], ACT.Copy).then_inc(max_copied, 1)

            def copy_out(count):
                act.wait_ge(out_done, ST * count)
                wait(act, out_turned, count - 1)
                nc.scalar.activation(o_raw[:], psum[:, OUTB, :], ACT.Copy).then_inc(out_copied, 1)

            def batch(b, first, last):
                for g in range(NG):
                    for st in range(ST):
                        step = ST * (NG * b + g) + st
                        for i in range(2):
                            act.wait_ge(keyed_done, 2 * step + i + 1)
                            if i == 0:
                                wait(act, out_done, step - PB + 1)
                            nc.scalar.activation(
                                probs[:, st % PB, 2 * i:2 * i + 2, :], psum[:, KEYED + 2 * i:KEYED + 2 * i + 2, :],
                                ACT.Exp, scale=SCALE).then_inc(exp_done, 1)
                        if st == LAG - 1 and not (first and g == 0):
                            copy_out(NG * b + g)
                        if st == TURN_MAX and not (last and g == NG - 1):
                            copy_max(NG * b + g + 2, slot(TURN_MAX, 4))

            copy_max(1, KEYED)
            batch(0, True, False)
            with act.Fori(1, B - 1) as b:
                batch(b, False, False)
            batch(B - 1, False, True)
            copy_out(NG * B)

        @block.vector
        def _(dve):
            def reduce(n, group, i, bank):
                dve.wait_ge(scores_done, n + 1)
                nc.vector.tensor_reduce(max_part[:, group % 2, i // 8, i // 2 % GH, i % 2:i % 2 + 1],
                                        psum[:, bank, :], AX_X, ALU.max).then_inc(scores_read, 1)

            def split_max(count, group):
                dve.wait_ge(scores_read, ITEMS * count)
                nc.vector.tensor_reduce(neg_max[:], max_part[:, group % 2], AX_X, ALU.max,
                                        negate=True).then_inc(max_ready, 1)
                dve.wait_ge(max_ready, count)
                wait(dve, max_turned, count - 1)
                nc.vector.tensor_copy(max_split[:, :, HI, :], neg_max[:]).then_inc(hi_ready, 1)
                dve.wait_ge(hi_ready, count)
                nc.vector.tensor_tensor(max_split[:, :, LO, :], neg_max[:], max_split[:, :, HI, :].bitcast(F32),
                                        ALU.subtract).then_inc(split_ready, 1)

            def normalise(count, b, g):
                dve.wait_ge(out_turned, count)
                turned = psum[:, slot(TURN_OUT, 4), :].rearrange("p (t j e) -> p t j e", t=LT, j=GH)
                nc.vector.reciprocal(recip[:], turned[:, :, :, E]).then_inc(recip_ready, 1)
                dve.wait_ge(recip_ready, count)
                wait(dve, attn_stored[g % 2], 16 * (NG // 2 * b + g // 2))
                dst = attn_out[:, g % 2].rearrange("p j t e -> p t j e")
                nc.vector.tensor_tensor(dst, turned[:, :, :, 0:E],
                                        recip[:].unsqueeze(3).to_broadcast([P, LT, GH, E]), ALU.mult).then_inc(out_ready, 1)

            for i in range(ITEMS):
                reduce(i, 0, i, MAXB + i % 3)
            split_max(1, 0)
            for i in range(ITEMS // 2):
                reduce(ITEMS + i, 1, i, MAXB + (ITEMS + i) % 3)

            def batch(b, first, last):
                for g in range(NG):
                    for st in range(ST):
                        step, step_in = ST * (NG * b + g) + st, ST * g + st
                        ahead = 1 if st < ST // 2 else 2
                        if not (last and g + ahead >= NG):
                            for i in range(4):
                                reduce(FIRST + 4 * step + i, g + ahead, (FIRST + 4 * step_in + i) % ITEMS, slot(st, i))
                        if st == TURN_OUT and not (first and g == 0):
                            normalise(NG * b + g, b, g - 1)
                        if st == 3 and not (last and g == NG - 1):
                            split_max(NG * b + g + 2, g + 1)

            batch(0, True, False)
            with dve.Fori(1, B - 1) as b:
                batch(b, False, False)
            batch(B - 1, False, True)
            normalise(NG * B, B, -1)

        @block.tensor
        def _(pe):
            def scores(g, i, bank):
                t, j, half = i // 8, i // 2 % GH, i % 2
                nc.tensor.matmul(psum[:, bank, :], q_stack[:, g, j, t * P:(t + 1) * P],
                                 k_stack[:, g, j, half * 512:(half + 1) * 512], start=True,
                                 stop=True).then_inc(scores_done, 1)

            def turn_max(count, bank):
                pe.wait_ge(split_ready, count)
                for t in range(LT):
                    last = nc.tensor.transpose(psum[0:2 * GH, bank, t * P:(t + 1) * P],
                                               max_split[:, t].rearrange("p a j -> p (a j)").bitcast(F32), ident[:])
                last.then_inc(max_turned, 1)

            def turn_out(count):
                pe.wait_ge(out_copied, count)
                queries = o_raw[:].rearrange("c (p t) -> c p t", t=LT)
                for t in range(LT):
                    last = nc.tensor.transpose(psum[:, slot(TURN_OUT, 4), t * P:(t + 1) * P], queries[:, :, t], ident[:])
                last.then_inc(out_turned, 1)

            def keyed(step, g, st, i):
                if not (isinstance(step, int) and step == 0):
                    pe.wait_ge(exp_done, 2 * step + i - 1)
                for j in (2 * i, 2 * i + 1):
                    last = nc.tensor.matmul(psum[:, KEYED + j, :], k_stack[:, g, j, st * P:(st + 1) * P],
                                            q_stack[:, g, j, :], start=True, stop=True)
                last.then_inc(keyed_done, 1)

            def weigh(step, g, st):
                pe.wait_ge(exp_done, 2 * (step + 1))
                for j in range(GH):
                    last = nc.tensor.matmul(psum[32 * j:32 * j + VW, OUTB, :], v_stack[:, g, st, j * VW:(j + 1) * VW],
                                            probs[:, st % PB, j, :], start=(st == 0), stop=(st == ST - 1),
                                            skip_group_check=True)
                last.then_inc(out_done, 1)

            pe.wait_ge(stack_loaded[0], 16 * LOADS)
            nc.tensor.matmul(psum[:, OUTB, :], q_stack[:, 0, 0, 0:P], q_stack[:, 0, 0, :], start=True, stop=True)
            for i in range(ITEMS):
                wait(pe, scores_read, i - 2)
                scores(0, i, MAXB + i % 3)
            pe.wait_ge(stack_loaded[1], 16 * LOADS)
            turn_max(1, KEYED)
            for i in range(ITEMS // 2):
                wait(pe, scores_read, ITEMS + i - 2)
                scores(1, i, MAXB + (ITEMS + i) % 3)

            def batch(b, first, last):
                for g in range(NG):
                    for st in range(ST):
                        step = ST * (NG * b + g) + st
                        if st == 0:
                            pe.wait_ge(max_placed, 32 * (NG * b + g + 1))
                        ahead = 1 if st < ST // 2 else 2
                        maxima = not (last and g + ahead >= NG)
                        if maxima and st == ST // 2:
                            pe.wait_ge(stack_loaded[(g + 2) % NG], 16 * LOADS * (b + 1 + (g + 2) // NG))

                        def item(i):
                            if not maxima:
                                return
                            n = FIRST + 4 * step + i
                            if (st - 1) % ST in EXTRAS and i < 2:
                                pe.wait_ge(scores_read, n - 1)
                            elif (st - 1) % ST in EXTRAS and i == 2:
                                if st == TURN_OUT + 1:
                                    wait(pe, out_ready, NG * b + g)
                                if st == TURN_MAX + 1:
                                    pe.wait_ge(max_copied, NG * b + g + 2)
                            else:
                                pe.wait_ge(scores_read, n - 2)
                            scores((g + ahead) % NG, (FIRST + 4 * (ST * g + st) + i) % ITEMS, slot(st, i))

                        keyed(step, g, st, 0)
                        item(0)
                        keyed(step, g, st, 1)
                        item(1)
                        item(2)
                        if not (first and g == 0 and st < LAG):
                            if st == LAG:
                                wait(pe, out_copied, NG * b + g)
                            weigh(step - LAG, (g if st >= LAG else g - 1) % NG, (st - LAG) % ST)
                        item(3)
                        if st == TURN_OUT and not (first and g == 0):
                            if maxima:
                                pe.wait_ge(scores_read, FIRST + 4 * step + 2)
                            else:
                                pe.wait_ge(out_ready, NG * b + g - 1)
                            turn_out(NG * b + g)
                        if st == TURN_MAX and not (last and g == NG - 1):
                            if maxima:
                                pe.wait_ge(scores_read, FIRST + 4 * step + 2)
                            turn_max(NG * b + g + 2, slot(TURN_MAX, 4))

            batch(0, True, False)
            with pe.Fori(1, B - 1) as b:
                batch(b, False, False)
            batch(B - 1, False, True)
            for lag in range(LAG, 0, -1):
                weigh(ST * NG * B - lag, NG - 1, ST - lag)
            pe.wait_ge(out_ready, NG * B - 1)
            turn_out(NG * B)


def feed_forward(nc, psum, ident, wo_t, wg1_t, attn_rows, w_raw, raw_loaded, x, bo, bg1, wg2, bg2, we, be, out):
    TOP = 8
    EXPERT, TURNED, SUMS = 0, 4, 6
    PER = 2 * LT
    with ExitStack() as ctx:
        def sb(name, shape, dt):
            return ctx.enter_context(nc.sbuf_tensor(name, shape, dt))

        def sem(name):
            return ctx.enter_context(nc.semaphore(name))

        w_t = sb("w_t", [P, 2, KC, NX, D], F32R)
        total = sb("total", [P, NT, D], F32)
        x_bias = sb("x_bias", [P, 2, LT, D], F32)
        attn = sb("attn", [P, 2, LT, D], F32)
        attn_t = sb("attn_t", [P, 2, KC, L], F32R)
        x2_norm = sb("x2_norm", [P, LT, D], F32)
        x2_t = [sb(f"x2_t{i}", [P, 2, KC, L], F32R) for i in range(2)]
        hidden = sb("hidden", [HID, L], F32)
        bo_row = sb("bo_row", [P, D], F32)
        bg1_col = sb("bg1_col", [HID, 1], F32)
        wg2_sb = sb("wg2_sb", [HID, NX], F32)
        bg2_row = sb("bg2_row", [P, NX], F32)
        be_sb = sb("be_sb", [NX, D], F32)
        stats2 = sb("stats2", [P, LT, 6], F32)
        moments2 = sb("moments2", [P, LT, 2], F32)
        var2 = sb("var2", [P, LT], F32)
        minus_half2 = sb("minus_half2", [P, LT], F32)
        rstd2 = sb("rstd2", [P, LT], F32)
        iota_x = sb("iota_x", [P, NX], F32)
        logits = sb("logits", [P, LT, NX], F32)
        shifted = sb("shifted", [P, LT, NX], F32)
        neg_top = sb("neg_top", [P, LT], F32)
        exps = sb("exps", [P, LT, NX], F32)
        exp_sum = sb("exp_sum", [P, LT], F32)
        sum_inv = sb("sum_inv", [P, LT], F32)
        probs = sb("route_probs", [P, LT, NX], F32)
        top = sb("top", [P, LT, TOP], F32)
        top_at = sb("top_at", [P, LT, TOP], U32)
        top_at_f = sb("top_at_f", [P, LT, 2], F32)
        picked = sb("picked", [P, 2, LT, NX], F32)
        gates = sb("gates", [P, 2, LT, NX], F32)
        gates_t = sb("gates_t", [NX, L], F32)

        small_loaded = sem("small_loaded")
        bo_loaded = sem("bo_loaded")
        consts_ready = sem("consts_ready")
        x_loaded = [sem(f"x2_loaded{i}") for i in range(2)]
        attn_loaded = [sem(f"attn_loaded{i}") for i in range(2)]
        bias_added = sem("bias_added")
        w_hi = sem("w_hi")
        w_lo = sem("w_lo")
        at_done = sem("at_done")
        at_hi = sem("at_hi")
        at_lo = sem("at_lo")
        proj_done = sem("oproj_done")
        total_ready = sem("total_ready")
        stats_done = sem("stats2_done")
        moments_done = sem("moments2_done")
        eps_added = sem("eps2_added")
        rstd_ready = sem("rstd2_ready")
        norm_ready = sem("norm2_ready")
        x2_done = sem("x2_done")
        x2_hi = sem("x2_hi")
        x2_lo = sem("x2_lo")
        hidden_done = sem("hidden_done")
        hidden_ready = sem("hidden_ready")
        logits_done = sem("logits_done")
        logits_ready = sem("logits_ready")
        neg_top_ready = sem("neg_top_ready")
        shifted_ready = sem("shifted_ready")
        exps_ready = sem("exps_ready")
        sum_ready = sem("sum_ready")
        inv_ready = sem("inv_ready")
        probs_ready = sem("probs_ready")
        top_ready = sem("top_ready")
        at_ready = sem("at_ready")
        at_f_ready = sem("at_f_ready")
        picked_ready = sem("picked_ready")
        gates_ready = sem("gates_ready")
        gates_turned = sem("gates_turned")
        gates_copied = sem("gates_copied")
        bias_done = sem("bias_done")
        bias_in = sem("bias_in")
        expert_done = sem("expert_done")
        expert_in = sem("expert_in")
        out_stored = sem("out_stored")

        SMALL = 4

        def pairs(eng, one, first, last):
            if last - first == 1:
                one(first)
            else:
                with eng.Fori(first, last) as p:
                    one(p)

        block = ctx.enter_context(nc.Block())

        @block.sync
        def _(sp):
            def load_attn(c):
                wait(sp, at_done, KC * (c - 1))
                sp.dma_start(attn[:, c % 2], attn_rows[c].rearrange("(t p) d -> p t d", p=P)).then_inc(
                    attn_loaded[c % 2], 16)

            def load_x(c):
                wait(sp, total_ready, 2 * (c - 1))
                sp.dma_start(x_bias[:, c % 2], x[c].rearrange("(t p) d -> p t d", p=P)).then_inc(x_loaded[c % 2], 16)

            def load_weights(p):
                sp.wait_ge(w_lo, p - RAW + 1)
                load_pair(sp, we, w_raw, raw_loaded, p)

            load_attn(0)
            load_x(0)
            sp.dma_start(bg1_col[:], bg1.rearrange("(h o) -> h o", o=1), allow_slow_non_contiguous=True).then_inc(small_loaded, 16)
            sp.dma_start(wg2_sb[:], wg2[:, 0:NX]).then_inc(small_loaded, 16)
            sp.dma_start(bg2_row[:], bg2[0:NX].partition_broadcast(P)).then_inc(small_loaded, 16)
            sp.dma_start(be_sb[:], be).then_inc(small_loaded, 16)
            load_attn(1)
            load_x(1)
            p = RAW
            for load in (load_attn, load_x, None, load_attn, load_x):
                load_weights(p)
                if load:
                    load(2 if p < RAW + 2 else 3)
                p += 1
            for p in range(p, PAIRS):
                load_weights(p)
            for c in range(B):
                sp.wait_ge(expert_in, PER * PAIRS * (c + 1))
                sp.dma_start(out[c].rearrange("(t p) d -> p t d", p=P),
                             total[:, LT * c:LT * (c + 1), :]).then_inc(out_stored, 16)
            sp.wait_ge(out_stored, 16 * B)

        @block.gpsimd
        def _(pool):
            pool.dma_start(bo_row[:], bo.partition_broadcast(P)).then_inc(bo_loaded, 16)
            nc.gpsimd.memset(minus_half2[:], -0.5).then_inc(consts_ready, 1)
            nc.gpsimd.iota(iota_x[:], pattern=[[1, NX]], base=0, channel_multiplier=0,
                           allow_small_or_imprecise_dtypes=True).then_inc(consts_ready, 1)
            pool.wait_ge(consts_ready, 1)
            pool.wait_ge(bo_loaded, 16)

            def add_bias(c):
                pool.wait_ge(x_loaded[c % 2], 16 * (c // 2 + 1))
                nc.gpsimd.tensor_tensor(x_bias[:, c % 2], x_bias[:, c % 2],
                                        bo_row[:].unsqueeze(1).to_broadcast([P, LT, D]), ALU.add).then_inc(bias_added, 1)

            def split_weights(p):
                pool.wait_ge(w_hi, p + 1)
                nc.gpsimd.tensor_tensor(w_t[:, LO, :, 2 * p:2 * p + 2, :], w_raw[:, p % RAW],
                                        w_t[:, HI, :, 2 * p:2 * p + 2, :].bitcast(F32), ALU.subtract).then_inc(w_lo, 1)

            def invert(c):
                pool.wait_ge(eps_added, c + 1)
                nc.gpsimd.tensor_tensor(rstd2[:], var2[:], minus_half2[:], ALU.pow).then_inc(rstd_ready, 1)

            add_bias(0)
            split_weights(0)
            invert(0)
            add_bias(1)
            for p in range(1, PAIRS // 2):
                split_weights(p)
            invert(1)
            for p in range(PAIRS // 2, PAIRS):
                split_weights(p)
            for c in range(2, B):
                add_bias(c)
                invert(c)

        @block.scalar
        def _(act):
            def round_weights(p):
                act.wait_ge(raw_loaded[p % RAW], 32 * (p // RAW + 1))
                nc.scalar.activation(w_t[:, HI, :, 2 * p:2 * p + 2, :], w_raw[:, p % RAW], ACT.Copy).then_inc(w_hi, 1)

            def round_attention(c):
                wait(act, proj_done, 2 * c)
                for k in range(KC):
                    act.wait_ge(at_done, KC * c + k + 1)
                    nc.scalar.activation(attn_t[:, HI, k, :], psum[:, TURNED + k, :], ACT.Copy).then_inc(at_hi, 1)

            def round_norm(c):
                wait(act, expert_done, LT * PAIRS * (c - 1))
                wait(act, hidden_done, c - 1)
                for k in range(KC):
                    act.wait_ge(x2_done, KC * c + k + 1)
                    nc.scalar.activation(x2_t[c % 2][:, HI, k, :], psum[:, TURNED + k, :], ACT.Copy).then_inc(x2_hi, 1)

            def gelu(c):
                act.wait_ge(hidden_done, c + 1)
                wait(act, logits_done, c)
                nc.scalar.activation(hidden[:], psum[0:HID, SUMS, :], ACT.Gelu, bias=bg1_col[:]).then_inc(hidden_ready, 1)

            def exp(c):
                act.wait_ge(shifted_ready, c + 1)
                nc.scalar.activation(exps[:], shifted[:], ACT.Exp).then_inc(exps_ready, 1)

            def copy_gates(c):
                act.wait_ge(gates_turned, c + 1)
                wait(act, bias_done, 2 * c)
                nc.scalar.activation(gates_t[:], psum[0:NX, TURNED, :], ACT.Copy).then_inc(gates_copied, 1)

            act.wait_ge(small_loaded, 16 * SMALL)
            round_weights(0)
            round_attention(0)
            round_weights(1)
            round_norm(0)
            gelu(0)
            exp(0)
            round_weights(2)
            round_weights(3)
            copy_gates(0)
            for c in range(1, B):
                round_attention(c)
                if c == 1:
                    round_weights(4)
                    round_weights(5)
                round_norm(c)
                if c == 1:
                    round_weights(6)
                    round_weights(7)
                gelu(c)
                if c == 1:
                    for p in range(8, PAIRS):
                        round_weights(p)
                exp(c)
                copy_gates(c)

        @block.vector
        def _(dve):
            def split_attention(c):
                for k in range(KC):
                    dve.wait_ge(at_hi, KC * c + k + 1)
                    nc.vector.tensor_tensor(attn_t[:, LO, k, :], psum[:, TURNED + k, :],
                                            attn_t[:, HI, k, :].bitcast(F32), ALU.subtract).then_inc(at_lo, 1)

            def residual(c):
                dve.wait_ge(bias_added, c + 1)
                for h in range(2):
                    dve.wait_ge(proj_done, 2 * c + h + 1)
                    t = LT * c + 2 * h
                    nc.vector.tensor_tensor(total[:, t:t + 2, :],
                                            psum[:, SUMS + h, :].rearrange("p (t d) -> p t d", t=2),
                                            x_bias[:, c % 2, 2 * h:2 * h + 2, :], ALU.add).then_inc(total_ready, 1)
                for t in range(LT):
                    dve.wait_ge(total_ready, 2 * c + t // 2 + 1)
                    nc.vector.bn_stats(stats2[:, t, :], total[:, LT * c + t, :]).then_inc(stats_done, 1)
                for t in range(LT):
                    dve.wait_ge(stats_done, LT * c + t + 1)
                    nc.vector.bn_aggr(moments2[:, t, :], stats2[:, t, :]).then_inc(moments_done, 1)
                dve.wait_ge(moments_done, LT * (c + 1))
                nc.vector.tensor_scalar(var2[:], moments2[:, :, 1], EPS, None, ALU.add).then_inc(eps_added, 1)
                dve.wait_ge(rstd_ready, c + 1)
                wait(dve, x2_done, KC * c)
                for t in range(LT):
                    nc.vector.tensor_scalar(x2_norm[:, t, :], total[:, LT * c + t, :], moments2[:, t, 0:1],
                                            rstd2[:, t:t + 1], ALU.subtract, ALU.mult).then_inc(norm_ready, 1)

            def split_norm(c):
                for k in range(KC):
                    dve.wait_ge(x2_hi, KC * c + k + 1)
                    nc.vector.tensor_tensor(x2_t[c % 2][:, LO, k, :], psum[:, TURNED + k, :],
                                            x2_t[c % 2][:, HI, k, :].bitcast(F32), ALU.subtract).then_inc(x2_lo, 1)

            def route(c):
                dve.wait_ge(logits_done, c + 1)
                nc.vector.tensor_tensor(logits[:], psum[:, SUMS + 1, 0:LT * NX].rearrange("p (t x) -> p t x", t=LT),
                                        bg2_row[:].unsqueeze(1).to_broadcast([P, LT, NX]),
                                        ALU.add).then_inc(logits_ready, 1)
                dve.wait_ge(logits_ready, c + 1)
                nc.vector.tensor_reduce(neg_top[:], logits[:], AX_X, ALU.max, negate=True).then_inc(neg_top_ready, 1)
                dve.wait_ge(neg_top_ready, c + 1)
                nc.vector.tensor_tensor(shifted[:], logits[:], neg_top[:].unsqueeze(2).to_broadcast([P, LT, NX]),
                                        ALU.add).then_inc(shifted_ready, 1)
                dve.wait_ge(exps_ready, c + 1)
                nc.vector.tensor_reduce(exp_sum[:], exps[:], AX_X, ALU.add).then_inc(sum_ready, 1)
                dve.wait_ge(sum_ready, c + 1)
                nc.vector.reciprocal(sum_inv[:], exp_sum[:]).then_inc(inv_ready, 1)
                dve.wait_ge(inv_ready, c + 1)
                nc.vector.tensor_tensor(probs[:], exps[:], sum_inv[:].unsqueeze(2).to_broadcast([P, LT, NX]),
                                        ALU.mult).then_inc(probs_ready, 1)
                dve.wait_ge(probs_ready, c + 1)
                for t in range(LT):
                    nc.vector.max(top[:, t, :], probs[:, t, :]).then_inc(top_ready, 1)
                for t in range(LT):
                    dve.wait_ge(top_ready, LT * c + t + 1)
                    nc.vector.max_index(top_at[:, t, :], top[:, t, :], probs[:, t, :]).then_inc(at_ready, 1)
                dve.wait_ge(at_ready, LT * (c + 1))
                nc.vector.tensor_copy(top_at_f[:], top_at[:, :, 0:2]).then_inc(at_f_ready, 1)
                dve.wait_ge(at_f_ready, c + 1)
                for i in range(2):
                    for t in range(LT):
                        nc.vector.tensor_scalar(picked[:, i, t, :], iota_x[:], top_at_f[:, t, i:i + 1],
                                                top[:, t, i:i + 1], ALU.is_equal, ALU.mult).then_inc(picked_ready, 1)
                dve.wait_ge(picked_ready, 2 * LT * (c + 1))
                nc.vector.tensor_tensor(gates[:, c % 2], picked[:, 0], picked[:, 1], ALU.add).then_inc(gates_ready, 1)

            def add_biases(c):
                if c == 0:
                    dve.wait_ge(expert_in, PER)
                for h in range(2):
                    dve.wait_ge(bias_done, 2 * c + h + 1)
                    t = LT * c + 2 * h
                    nc.vector.tensor_tensor(total[:, t:t + 2, :], total[:, t:t + 2, :],
                                            psum[:, SUMS + h, :].rearrange("p (t d) -> p t d", t=2),
                                            ALU.add).then_inc(bias_in, 1)

            def experts(c, p):
                if isinstance(p, int) and p == 0:
                    dve.wait_ge(gates_ready, c + 1)
                before = PER * (PAIRS * c + p)
                for t in range(0, LT, 2):
                    for e in range(2):
                        for u in (t, t + 1):
                            if e == 0:
                                dve.wait_ge(expert_done, LT * (PAIRS * c + p) + u + 1)
                            wait(dve, expert_in, before + 2 * t + (u - t) + 1 - (0 if e else PER - 2))
                            nc.vector.scalar_tensor_tensor(
                                out=total[:, LT * c + u, :], in0=psum[:, EXPERT + u, e * D:(e + 1) * D],
                                scalar=gates[:, c % 2, u, bass.ds(2 * p + e, 1)], in1=total[:, LT * c + u, :],
                                op0=ALU.mult, op1=ALU.add).then_inc(expert_in, 1)

            dve.wait_ge(small_loaded, 16 * SMALL)
            dve.wait_ge(consts_ready, 2)
            split_attention(0)
            residual(0)
            split_norm(0)
            route(0)
            for c in range(B):
                ahead = c + 1 < B
                def run(first, last):
                    pairs(dve, lambda p: experts(c, p), first, last)
                if c == 0:
                    run(0, 1)
                    add_biases(0)
                    dve.wait_ge(bias_in, 2)
                    split_attention(1)
                    run(1, 2)
                else:
                    if ahead:
                        split_attention(c + 1)
                    dve.wait_ge(bias_in, 2 * (c + 1))
                    run(0, 1)
                    run(1, 2)
                if not ahead:
                    run(2, PAIRS)
                    continue
                residual(c + 1)
                run(2, 4)
                split_norm(c + 1)
                run(4, 6)
                run(6, 7)
                route(c + 1)
                run(7, 9)
                run(9, PAIRS)
                add_biases(c + 1)

        @block.tensor
        def _(pe):
            def turn_attention(c):
                pe.wait_ge(attn_loaded[c % 2], 16 * (c // 2 + 1))
                wait(pe, gates_copied, c)
                wait(pe, x2_lo, KC * c)
                for k in range(KC):
                    for t in range(LT):
                        last = nc.tensor.transpose(psum[:, TURNED + k, t * P:(t + 1) * P],
                                                   attn[:, c % 2, t, k * P:(k + 1) * P], ident[:])
                    last.then_inc(at_done, 1)

            def project_out(c):
                pe.wait_ge(at_lo, KC * (c + 1))
                for h in range(2):
                    wait(pe, bias_in, 2 * (c - 1) + h + 1)
                    for u in range(2):
                        t = 2 * h + u
                        for m, (a, w, k) in enumerate(TERMS):
                            last = nc.tensor.matmul(psum[:, SUMS + h, u * D:(u + 1) * D],
                                                    attn_t[:, a, k, t * P:(t + 1) * P], wo_t[:, w, k, :],
                                                    start=(m == 0), stop=(m == len(TERMS) - 1))
                    last.then_inc(proj_done, 1)

            def turn_norm(c):
                pe.wait_ge(norm_ready, LT * (c + 1))
                for k in range(KC):
                    for t in range(LT):
                        last = nc.tensor.transpose(psum[:, TURNED + k, t * P:(t + 1) * P],
                                                   x2_norm[:, t, k * P:(k + 1) * P], ident[:])
                    last.then_inc(x2_done, 1)

            def hide(c):
                pe.wait_ge(x2_lo, KC * (c + 1))
                for m, (a, w, k) in enumerate(TERMS):
                    last = nc.tensor.matmul(psum[:, SUMS, :], wg1_t[:, w, k, :], x2_t[c % 2][:, a, k, :],
                                            start=(m == 0), stop=(m == len(TERMS) - 1))
                last.then_inc(hidden_done, 1)

            def score(c):
                pe.wait_ge(hidden_ready, c + 1)
                for t in range(LT):
                    last = nc.tensor.matmul(psum[:, SUMS + 1, t * NX:(t + 1) * NX], hidden[:, t * P:(t + 1) * P],
                                            wg2_sb[:], start=True, stop=True)
                last.then_inc(logits_done, 1)

            def turn_gates(c):
                pe.wait_ge(gates_ready, c + 1)
                for t in range(LT):
                    last = nc.tensor.transpose(psum[0:NX, TURNED, t * P:(t + 1) * P], gates[:, c % 2, t, :], ident[:])
                last.then_inc(gates_turned, 1)

            def bias(c):
                pe.wait_ge(gates_copied, c + 1)
                for h in range(2):
                    for u in range(2):
                        t = 2 * h + u
                        last = nc.tensor.matmul(psum[:, SUMS + h, u * D:(u + 1) * D], gates_t[:, t * P:(t + 1) * P],
                                                be_sb[:], start=True, stop=True)
                    last.then_inc(bias_done, 1)

            def experts(c, p):
                if c == 0:
                    pe.wait_ge(w_lo, p + 1)
                for t in range(LT):
                    wait(pe, expert_in, PER * (PAIRS * c + p - 1) + 4 * (t // 2 + 1))
                    for m, (a, w, k) in enumerate(TERMS):
                        last = nc.tensor.matmul(psum[:, EXPERT + t, :], x2_t[c % 2][:, a, k, t * P:(t + 1) * P],
                                                w_t[:, w, k, bass.ds(2 * p, 2), :], start=(m == 0),
                                                stop=(m == len(TERMS) - 1))
                    last.then_inc(expert_done, 1)

            pe.wait_ge(small_loaded, 16 * SMALL)
            turn_attention(0)
            project_out(0)
            turn_norm(0)
            hide(0)
            score(0)
            for c in range(B):
                ahead = c + 1 < B
                def run(first, last):
                    pairs(pe, lambda p: experts(c, p), first, last)
                if c == 0:
                    run(0, 1)
                    turn_gates(0)
                    bias(0)
                    turn_attention(1)
                    run(1, 2)
                else:
                    if ahead:
                        turn_attention(c + 1)
                    run(0, 2)
                if not ahead:
                    run(2, PAIRS)
                    continue
                project_out(c + 1)
                run(2, 4)
                turn_norm(c + 1)
                run(4, 6)
                hide(c + 1)
                run(6, 7)
                score(c + 1)
                run(7, 9)
                turn_gates(c + 1)
                run(9, PAIRS)
                bias(c + 1)


_INS = ['x', 'ctx_1024', 'L0_xattn_Wq', 'L0_xattn_bq', 'L0_xattn_Wo', 'L0_xattn_bo', 'L0_ffn_wg1', 'L0_ffn_bg1',
        'L0_ffn_wg2', 'L0_ffn_bg2', 'L0_ffn_We', 'L0_ffn_be']
_OUT = ((B, L, D), 'float32')


def kernel(**inputs):
    import numpy as _np
    import concourse.bacc as _bacc
    from concourse import mybir as _mybir
    from concourse.bass_utils import run_bass_kernel_spmd as _run

    nc = _bacc.Bacc("TRN2", target_bir_lowering=False, num_devices=1)
    arrays, args = {}, []
    for name in _INS:
        a = _np.ascontiguousarray(inputs[name])
        arrays[f"in_{name}_dram"] = a
        args.append(nc.dram_tensor(f"in_{name}_dram", a.shape, _mybir.dt.from_np(a.dtype), kind="ExternalInput").ap())
    args.append(nc.dram_tensor("out_dram", _OUT[0], _mybir.dt.from_np(_np.dtype(_OUT[1])), kind="ExternalOutput").ap())
    mixed_kernel(nc, *args)
    r = _run(nc, [arrays], core_ids=[0])
    return r.results[0]["out_dram"]
```

```python
from contextlib import ExitStack

import concourse.bass as bass
from concourse import mybir

ALU = mybir.AluOpType
ACT = mybir.ActivationFunctionType
AX_X = mybir.AxisListType.X
F32 = mybir.dt.float32
F32R = mybir.dt.float32r
U32 = mybir.dt.uint32

P = 128
B, L, S, D = 4, 512, 1024, 256
H = 16
E = D // H
KC = D // P
NX = 20
HID = D // 4
GH = 4
NG = H // GH
LT = L // P
ST = S // P
NT = B * LT
SCALE = float(E) ** -0.5
EPS = 1e-5
VW = E + 1
PAIRS = NX // 2
PER_GROUP = GH * S // (2 * KC * 2 * D)
LOADS = 8
RAW = 3

Q_SLABS = (0, 0, 1)
K_SLABS = (0, 1, 0)
MROW = 3 * E
HI, LO = 0, 1
TERMS = [(a, w, k) for a, w in ((HI, HI), (LO, HI), (HI, LO)) for k in range(KC)]


def wait(eng, sem, value):
    if not isinstance(value, int) or value > 0:
        eng.wait_ge(sem, value)


def mixed_kernel(nc, x, ctx_in, wq, bq, wo, bo, wg1, bg1, wg2, bg2, we, be, out):
    q_parts = nc.dram_tensor("q_parts", [B, 2, NG, GH, E, L], F32, kind="Internal").ap()
    k_parts = nc.dram_tensor("k_parts", [B, 2, NG, GH, E, S], F32, kind="Internal").ap()
    attn_rows = nc.dram_tensor("attn_rows", [B, L, D], F32, kind="Internal").ap()
    v_parts = nc.dram_tensor("v_parts", [B, NG, P, ST, GH * VW], F32, kind="Internal").ap()

    with ExitStack() as whole:
        def kept(name, shape, dt):
            return whole.enter_context(nc.sbuf_tensor(name, shape, dt))

        psum = whole.enter_context(nc.psum_tensor("psum", [P, 8, 512], F32))
        ident = kept("ident", [P, P], F32)
        wo_t = kept("wo_t", [P, 2, KC, D], F32R)
        wg1_t = kept("wg1_t", [P, 2, KC, P], F32R)
        w_t = kept("w_t", [P, PAIRS, 2, KC, 2 * D], F32R)
        k_stack = w_t[:, 0:NG * PER_GROUP].rearrange("p n a k d -> p (n a k d)").rearrange(
            "p (g j s) -> p g j s", g=NG, j=GH)
        v_stack = w_t[:, NG * PER_GROUP:PAIRS].rearrange("p n a k d -> p (n a k d)")[
            :, 0:NG * ST * GH * VW].bitcast(F32).rearrange("p (g t v) -> p g t v", g=NG, t=ST)
        q_stack = kept("q_stack", [P, NG, GH, L], F32R)
        zero_rows = kept("zero_rows", [2, P], F32)
        stack_loaded = [whole.enter_context(nc.semaphore(f"stack_loaded{g}")) for g in range(NG)]

        def load_stack(sp, b, g):
            for r, part in enumerate(Q_SLABS):
                sp.dma_start(q_stack[r * E:(r + 1) * E, g, :, :].bitcast(F32),
                             q_parts[b, part, g].rearrange("j e l -> e j l")).then_inc(stack_loaded[g], 16)
            for r, part in enumerate(K_SLABS):
                sp.dma_start(k_stack[r * E:(r + 1) * E, g, :, :].bitcast(F32),
                             k_parts[b, part, g].rearrange("j e s -> e j s")).then_inc(stack_loaded[g], 16)
            sp.dma_start(q_stack[MROW:MROW + 2, g].rearrange("p j (n l) -> p (j n) l", l=P).bitcast(F32),
                         zero_rows[:].unsqueeze(1).to_broadcast([2, GH * L // P, P])).then_inc(stack_loaded[g], 16)
            sp.dma_start(v_stack[:, g, :, :], v_parts[b, g]).then_inc(stack_loaded[g], 16)

        stored = [[whole.enter_context(nc.semaphore(f"stored{n}{c}")) for c in range(KC)] for n in range(S // L + 1)]
        v_stored = [whole.enter_context(nc.semaphore(f"v_stored{i}")) for i in range(S // L)]

        def wait_stored(sp, batches):
            for by_chunk in stored:
                for done in by_chunk:
                    sp.wait_ge(done, 16 * batches)
            for done in v_stored:
                sp.wait_ge(done, 16 * batches)

        project(nc, psum, ident, wo_t, wg1_t, q_stack, k_stack, zero_rows, load_stack, stored, v_stored, wait_stored,
                x, ctx_in, wq, bq, wo, wg1, q_parts, k_parts, v_parts)
        attend_and_feed(nc, psum, ident, wo_t, wg1_t, w_t, q_stack, k_stack, v_stack, stack_loaded, load_stack,
                        wait_stored, attn_rows, x, bo, bg1, wg2, bg2, we, be, out)


def load_pair(sp, we, w_raw, raw_loaded, p):
    for i in range(2):
        sp.dma_start(w_raw[:, p % RAW, :, i, :], we[2 * p + i].rearrange("(k p) o -> p k o", p=P)).then_inc(
            raw_loaded[p % RAW], 16)


def project(nc, psum, ident, wo_t, wg1_t, q_stack, k_stack, zero_rows, load_stack, stored, v_stored, wait_stored,
            x, ctx_in, wq, bq, wo, wg1, q_parts, k_parts, v_parts):
    TILES = LT
    CH = S // L
    CHUNKS = CH + 1
    NTR = CHUNKS * KC
    TURNED = (0, 6, 0)
    PROJ, VALS = 2, (4, 6)
    with ExitStack() as ctx:
        def sb(name, shape, dt):
            return ctx.enter_context(nc.sbuf_tensor(name, shape, dt))

        def sem(name):
            return ctx.enter_context(nc.semaphore(name))

        w_nat = sb("w_nat", [P, 2, KC, D], F32)
        g_nat = sb("g_nat", [P, KC, P], F32)
        wq_t = sb("wq_t", [P, 2, KC, D], F32R)
        bq_col = sb("bq_col", [P, KC], F32)
        x_in = sb("x_in", [P, TILES, D], F32)
        c_in = [sb(f"c_in{i}", [P, TILES, D], F32) for i in range(CH)]
        stats = sb("stats", [P, TILES, 6], F32)
        mean_gap = sb("mean_gap", [P, TILES], F32)
        squares = sb("squares", [P, TILES], F32)
        gap_square = sb("gap_square", [P, TILES], F32)
        mean = sb("mean", [P, TILES], F32)
        var = sb("var", [P, TILES], F32)
        var_eps = sb("var_eps", [P, TILES], F32)
        minus_half = sb("minus_half", [P, TILES], F32)
        rstd = sb("rstd", [P, TILES], F32)
        one_row = sb("one_row", [2, P], F32)
        tok_t = [sb(f"tok_t{n}", [P, 2, KC, L], F32R) for n in range(CHUNKS)]
        k_full = [[sb(f"k_full{i}{c}", [P, L], F32) for c in range(KC)] for i in range(CH)]
        stage = [[sb(f"stage{n}{c}", [P, 2, L], F32R) for c in range(KC)] for n in range(CHUNKS)]
        v_stage = [sb(f"v_stage{i}", [P, NG, TILES, GH * VW], F32) for i in range(CH)]

        wq_loaded = sem("wq_loaded")
        consts_loaded = sem("consts_loaded")
        g_zeroed = sem("g_zeroed")
        g_loaded = sem("g_loaded")
        ident_zeroed = sem("ident_zeroed")
        ident_ready = sem("ident_ready")
        filled = sem("filled")
        cleared = sem("cleared")
        ones_set = sem("ones_set")
        wt_done = sem("wt_done")
        wt_hi = sem("wt_hi")
        wt_lo = sem("wt_lo")
        x_loaded = sem("x_loaded")
        c_loaded = [sem(f"c_loaded{i}") for i in range(CH)]
        stats_done = sem("stats_done")
        gap_done = sem("gap_done")
        squares_done = sem("squares_done")
        mean_ready = sem("mean_ready")
        square_done = sem("square_done")
        var_done = sem("var_done")
        eps_added = sem("eps_added")
        rstd_ready = sem("rstd_ready")
        norm_ready = sem("norm_ready")
        tok_done = sem("tok_done")
        tok_hi = sem("tok_hi")
        tok_lo = sem("tok_lo")
        proj_done = sem("proj_done")
        k_ready = sem("k_ready")
        proj_hi = sem("proj_hi")
        proj_lo = sem("proj_lo")
        v_done = sem("v_done")
        v_ready = sem("v_ready")

        block = ctx.enter_context(nc.Block())

        @block.sync
        def _(sp):
            sp.dma_start(w_nat[:, 0], wq.rearrange("(c p) i -> p c i", p=P)).then_inc(wq_loaded, 16)
            sp.dma_start(bq_col[:], bq.rearrange("(c p) -> p c", p=P),
                         allow_slow_non_contiguous=True).then_inc(consts_loaded, 16)
            sp.dma_start(w_nat[:, 1], wo.rearrange("(c p) i -> p c i", p=P)).then_inc(consts_loaded, 16)
            sp.wait_ge(g_zeroed, 1)
            sp.dma_start(g_nat[:, :, 0:HID], wg1.rearrange("(k p) h -> p k h", p=P)).then_inc(g_loaded, 16)

            def store_parts(b, n):
                for c in range(KC):
                    sp.wait_ge(proj_lo, NTR * b + KC * n + c + 1)
                    rows = slice(c * P, (c + 1) * P)
                    if n == CH:
                        dst = q_parts[b].rearrange("a g j e l -> (g j e) a l")[rows]
                    else:
                        dst = k_parts[b].rearrange("a g j e l -> (g j e) a l")[rows, :, n * L:(n + 1) * L]
                    sp.dma_start(dst, stage[n][c][:].bitcast(F32)).then_inc(stored[n][c], 16)

            def store_values(b, i):
                sp.wait_ge(v_ready, 2 * TILES * b + TILES * (i + 1))
                dst = v_parts[b, :, :, i * TILES:(i + 1) * TILES, :].rearrange("g p t v -> p g t v")
                sp.dma_start(dst, v_stage[i][:]).then_inc(v_stored[i], 16)

            def batch(b):
                for i in range(CH):
                    store_parts(b, i)
                    store_values(b, i)
                store_parts(b, CH)

            batch(0)
            sp.wait_ge(cleared, 4)
            sp.dma_start(k_stack[MROW:MROW + 2].rearrange("p g j s -> p (g j s)").rearrange(
                "p (n l) -> p n l", l=P).bitcast(F32), one_row[:].unsqueeze(1).to_broadcast([2, NG * GH * S // P, P])
            ).then_inc(ones_set, 16)
            with sp.Fori(1, B - 1) as b:
                batch(b)
            wait_stored(sp, B - 1)
            load_stack(sp, 0, 0)
            batch(B - 1)
            sp.wait_ge(ones_set, 16)

        @block.gpsimd
        def _(pool):
            nc.gpsimd.memset(ident[:], 0.0).then_inc(ident_zeroed, 1)
            nc.gpsimd.memset(g_nat[:], 0.0).then_inc(g_zeroed, 1)
            pool.wait_ge(ident_zeroed, 1)
            nc.gpsimd.affine_select(out=ident[:], in_=ident[:], compare_op=ALU.not_equal, fill=1.0, base=0,
                                    pattern=[[-1, P]], channel_multiplier=1).then_inc(ident_ready, 1)
            nc.gpsimd.memset(minus_half[:], -0.5).then_inc(filled, 1)
            for i in range(CH):
                nc.gpsimd.memset(v_stage[i][:], 1.0).then_inc(filled, 1)
            pool.wait_ge(filled, 1)

            def batch(b):
                pool.wait_ge(eps_added, b + 1)
                nc.gpsimd.tensor_tensor(rstd[:], var_eps[:], minus_half[:], ALU.pow).then_inc(rstd_ready, 1)

            nc.gpsimd.memset(zero_rows[:], 0.0).then_inc(cleared, 1)
            nc.gpsimd.memset(one_row[:], 1.0).then_inc(cleared, 1)
            nc.gpsimd.memset(q_stack[:].bitcast(F32), 0.0).then_inc(cleared, 1)
            batch(0)
            nc.gpsimd.memset(k_stack[:].bitcast(F32), 0.0).then_inc(cleared, 1)
            with pool.Fori(1, B) as b:
                batch(b)

        @block.vector
        def _(dve):
            def split_weights(n, dst):
                dve.wait_ge(wt_hi, n + 1)
                src = psum[:, 2 + n, :].rearrange("p (k o) -> p k o", k=KC)
                nc.vector.tensor_tensor(dst[:, LO], src, dst[:, HI].bitcast(F32), ALU.subtract).then_inc(wt_lo, 1)

            def split_tok(b, n):
                for k in range(KC):
                    dve.wait_ge(tok_hi, NTR * b + KC * n + k + 1)
                    nc.vector.tensor_tensor(tok_t[n][:, LO, k, :], psum[:, TURNED[n] + k, :],
                                            tok_t[n][:, HI, k, :].bitcast(F32), ALU.subtract).then_inc(tok_lo, 1)

            def split_proj(b, n):
                for c in range(KC):
                    dve.wait_ge(proj_hi, NTR * b + KC * n + c + 1)
                    if n < CH:
                        nc.vector.tensor_tensor(stage[n][c][:, LO, :], k_full[n][c][:],
                                                stage[n][c][:, HI, :].bitcast(F32), ALU.subtract).then_inc(proj_lo, 1)
                    else:
                        nc.vector.scalar_tensor_tensor(
                            out=stage[n][c][:, LO, :], in0=psum[:, PROJ + c, :], scalar=bq_col[:, c:c + 1],
                            in1=stage[n][c][:, HI, :].bitcast(F32), op0=ALU.add, op1=ALU.subtract).then_inc(proj_lo, 1)

            def take_values(b, i):
                wait(dve, v_stored[i], 16 * b)
                for t in range(TILES):
                    dve.wait_ge(v_done, 2 * CH * b + 2 * i + t // 2 + 1)
                    dst = v_stage[i][:, :, t, :].rearrange("p g (j v) -> p g j v", j=GH)[:, :, :, 0:E]
                    src = psum[:, VALS[i] + t // 2, (t % 2) * D:(t % 2 + 1) * D]
                    nc.vector.tensor_copy(dst, src.rearrange("p (g j e) -> p g j e", g=NG, j=GH)).then_inc(v_ready, 1)

            def layer_norm(b):
                dve.wait_ge(x_loaded, 16 * (b + 1))
                for t in range(TILES):
                    nc.vector.bn_stats(stats[:, t, :], x_in[:, t, :]).then_inc(stats_done, 1)
                dve.wait_ge(stats_done, TILES * (b + 1))
                nc.vector.tensor_tensor(mean_gap[:], stats[:, :, 1], stats[:, :, 4], ALU.subtract).then_inc(gap_done, 1)
                nc.vector.tensor_tensor(squares[:], stats[:, :, 2], stats[:, :, 5], ALU.add).then_inc(squares_done, 1)
                dve.wait_ge(gap_done, b + 1)
                nc.vector.scalar_tensor_tensor(out=mean[:], in0=mean_gap[:], scalar=-0.5, in1=stats[:, :, 1],
                                               op0=ALU.mult, op1=ALU.add).then_inc(mean_ready, 1)
                nc.vector.scalar_tensor_tensor(out=gap_square[:], in0=mean_gap[:], scalar=0.25, in1=mean_gap[:],
                                               op0=ALU.mult, op1=ALU.mult).then_inc(square_done, 1)
                dve.wait_ge(squares_done, b + 1)
                dve.wait_ge(square_done, b + 1)
                nc.vector.scalar_tensor_tensor(out=var[:], in0=squares[:], scalar=1.0 / D, in1=gap_square[:],
                                               op0=ALU.mult, op1=ALU.add).then_inc(var_done, 1)
                dve.wait_ge(var_done, b + 1)
                nc.vector.tensor_scalar(var_eps[:], var[:], EPS, None, ALU.add).then_inc(eps_added, 1)
                dve.wait_ge(mean_ready, b + 1)
                dve.wait_ge(rstd_ready, b + 1)
                for t in range(TILES):
                    nc.vector.tensor_scalar(x_in[:, t, :], x_in[:, t, :], mean[:, t:t + 1], rstd[:, t:t + 1],
                                            ALU.subtract, ALU.mult).then_inc(norm_ready, 1)

            def batch(b, first):
                split_tok(b, 0)
                if first:
                    split_weights(1, wo_t)
                    dve.wait_ge(wt_hi, 3)
                    nc.vector.tensor_tensor(wg1_t[:, LO], g_nat[:], wg1_t[:, HI].bitcast(F32),
                                            ALU.subtract).then_inc(wt_lo, 1)
                else:
                    split_proj(b - 1, 2)
                split_tok(b, 1)
                layer_norm(b)
                split_proj(b, 0)
                split_proj(b, 1)
                split_tok(b, 2)
                take_values(b, 0)
                take_values(b, 1)

            split_weights(0, wq_t)
            dve.wait_ge(consts_loaded, 32)
            dve.wait_ge(filled, CHUNKS)
            batch(0, True)
            with dve.Fori(1, B) as b:
                batch(b, False)
            split_proj(B - 1, 2)

        @block.scalar
        def _(act):
            def load_tokens(b, n):
                src = x[b] if n == CH else ctx_in[b, n * L:(n + 1) * L, :]
                dst, done = (x_in, x_loaded) if n == CH else (c_in[n], c_loaded[n])
                act.dma_start(dst[:], src.rearrange("(t p) d -> p t d", p=P)).then_inc(done, 16)

            def round_weights(n, dst):
                act.wait_ge(wt_done, n + 1)
                src = psum[:, 2 + n, :].rearrange("p (k o) -> p k o", k=KC)
                nc.scalar.activation(dst[:, HI], src, ACT.Copy).then_inc(wt_hi, 1)

            def round_tok(b, n, last):
                for k in range(KC):
                    act.wait_ge(tok_done, NTR * b + KC * n + k + 1)
                    nc.scalar.activation(tok_t[n][:, HI, k, :], psum[:, TURNED[n] + k, :], ACT.Copy).then_inc(tok_hi, 1)
                if not last:
                    load_tokens(b + 1, n)

            def round_proj(b, n):
                for c in range(KC):
                    act.wait_ge(proj_done, NTR * b + KC * n + c + 1)
                    if n < CH:
                        wait(act, v_done, 2 * (CH * (b - 1) + n + 1))
                        wait(act, proj_lo, NTR * (b - 1) + KC * n + c + 1)
                        nc.scalar.activation(k_full[n][c][:], psum[:, PROJ + c, :], ACT.Identity,
                                             bias=bq_col[:, c:c + 1]).then_inc(k_ready, 1)
                for c in range(KC):
                    wait(act, stored[n][c], 16 * b)
                    if n < CH:
                        act.wait_ge(k_ready, KC * (CH * b + n) + c + 1)
                        nc.scalar.activation(stage[n][c][:, HI, :], k_full[n][c][:], ACT.Copy).then_inc(proj_hi, 1)
                    else:
                        nc.scalar.activation(stage[n][c][:, HI, :], psum[:, PROJ + c, :], ACT.Identity,
                                             bias=bq_col[:, c:c + 1]).then_inc(proj_hi, 1)

            def batch(b, first, last):
                round_tok(b, 0, last)
                if first:
                    round_weights(1, wo_t)
                    act.wait_ge(g_loaded, 16)
                    nc.scalar.activation(wg1_t[:, HI], g_nat[:], ACT.Copy).then_inc(wt_hi, 1)
                else:
                    round_proj(b - 1, 2)
                round_tok(b, 1, last)
                round_proj(b, 0)
                round_proj(b, 1)
                round_tok(b, 2, last)

            for n in range(CHUNKS):
                load_tokens(0, n)
            round_weights(0, wq_t)
            act.wait_ge(consts_loaded, 32)
            batch(0, True, False)
            with act.Fori(1, B - 1) as b:
                batch(b, False, False)
            batch(B - 1, False, True)
            round_proj(B - 1, 2)

        @block.tensor
        def _(pe):
            def turn_weights(n):
                for k in range(KC):
                    for c in range(KC):
                        last = nc.tensor.transpose(psum[:, 2 + n, k * D + c * P:k * D + (c + 1) * P],
                                                   w_nat[:, n, c, k * P:(k + 1) * P], ident[:])
                last.then_inc(wt_done, 1)

            def turn_tokens(b, n):
                if n == CH:
                    pe.wait_ge(norm_ready, TILES * (b + 1))
                    src = x_in
                    pe.wait_ge(tok_lo, NTR * b + KC)
                else:
                    pe.wait_ge(c_loaded[n], 16 * (b + 1))
                    src = c_in[n]
                    wait(pe, tok_lo, NTR * b)
                    if n == 1:
                        wait(pe, v_ready, TILES * CH * b)
                for k in range(KC):
                    for t in range(TILES):
                        last = nc.tensor.transpose(psum[:, TURNED[n] + k, t * P:(t + 1) * P],
                                                   src[:, t, k * P:(k + 1) * P], ident[:])
                    last.then_inc(tok_done, 1)

            def projections(b, n):
                pe.wait_ge(tok_lo, NTR * b + KC * (n + 1))
                if isinstance(b, int) and b == 0 and n == 0:
                    pe.wait_ge(wt_lo, 2)
                for c in range(KC):
                    if n == 0:
                        wait(pe, proj_lo, NTR * b - KC + c + 1)
                    else:
                        pe.wait_ge(k_ready, KC * (CH * b + n - 1) + c + 1)
                    for m, (a, w, k) in enumerate(TERMS):
                        last = nc.tensor.matmul(psum[:, PROJ + c, :], wq_t[:, w, k, c * P:(c + 1) * P],
                                                tok_t[n][:, a, k, :], start=(m == 0), stop=(m == len(TERMS) - 1))
                    last.then_inc(proj_done, 1)

            def values(b, i):
                pe.wait_ge(k_ready, KC * (CH * b + i + 1))
                for pr in range(2):
                    wait(pe, v_ready, TILES * (CH * (b - 1) + i) + 2 * (pr + 1))
                    for t in (2 * pr, 2 * pr + 1):
                        for c in range(KC):
                            at = (t % 2) * D + c * P
                            last = nc.tensor.transpose(psum[:, VALS[i] + pr, at:at + P],
                                                       k_full[i][c][:, t * P:(t + 1) * P], ident[:])
                    last.then_inc(v_done, 1)

            def batch(b, first):
                turn_tokens(b, 0)
                if first:
                    pe.wait_ge(consts_loaded, 32)
                    turn_weights(1)
                else:
                    projections(b - 1, 2)
                turn_tokens(b, 1)
                projections(b, 0)
                projections(b, 1)
                turn_tokens(b, 2)
                values(b, 0)
                values(b, 1)

            pe.wait_ge(ident_ready, 1)
            pe.wait_ge(wq_loaded, 16)
            turn_weights(0)
            pe.wait_ge(wt_lo, 1)
            batch(0, True)
            with pe.Fori(1, B) as b:
                batch(b, False)
            projections(B - 1, 2)


def attend_and_feed(nc, psum, ident, wo_t, wg1_t, w_t, q_stack, k_stack, v_stack, stack_loaded, load_stack,
                    wait_stored, attn_rows, x, bo, bg1, wg2, bg2, we, be, out):
    ITEMS = LT * GH * 2
    PB = 2
    LAG = 1
    TOP = 8
    STEP = 32
    GATE_ROWS = 2 * STEP + NX
    EXPERT, TURNED, LOGITS = 0, 4, 5
    SUMS, FIRST_SUMS = (6, 7), (6, 5)
    PER = 2 * LT
    with ExitStack() as ctx:
        def sb(name, shape, dt):
            return ctx.enter_context(nc.sbuf_tensor(name, shape, dt))

        def sem(name):
            return ctx.enter_context(nc.semaphore(name))

        probs = sb("probs", [P, PB, GH, L], F32)
        max_part = sb("max_part", [P, 2, GH, LT, 2], F32)
        neg_max = sb("neg_max", [P, GH, LT], F32)
        max_split = sb("max_split", [P, 2, GH, LT], F32R)
        max_rows = sb("max_rows", [2 * GH * LT, P], F32)
        o_raw = sb("o_raw", [P, L], F32)
        recip = sb("recip", [P, LT, GH], F32)
        attn_out = sb("attn_out", [P, 2, GH, LT, E], F32)

        w_raw = sb("w_raw", [P, RAW, KC, 2, D], F32)
        total = sb("total", [P, NT, D], F32)
        attn = [q_stack[:, 1, 2 * i:2 * i + 2].rearrange("p j l -> p (j l)").bitcast(F32).rearrange(
            "p (t d) -> p t d", t=LT) for i in range(2)]
        x_again = sb("x_again", [P, LT, D], F32)
        x_bias = sb("x_bias", [P, LT, D], F32)
        attn_t = sb("attn_t", [P, 2, KC, L], F32R)
        x2_norm = sb("x2_norm", [P, LT, D], F32)
        x2_t = [sb("x2_t", [P, 2, KC, L], F32R), q_stack[:, 0].rearrange("p (a k) l -> p a k l", a=2)]
        hidden = sb("hidden", [HID, L], F32)
        bo_row = sb("bo_row", [P, D], F32)
        bg1_col = sb("bg1_col", [HID, 1], F32)
        wg2_sb = sb("wg2_sb", [HID, NX], F32)
        bg2_row = sb("bg2_row", [P, NX], F32)
        be_raw = sb("be_raw", [GATE_ROWS, D], F32)
        stats2 = sb("stats2", [P, LT, 6], F32)
        moments2 = sb("moments2", [P, LT, 2], F32)
        var2 = sb("var2", [P, LT], F32)
        minus_half2 = sb("minus_half2", [P, LT], F32)
        rstd2 = sb("rstd2", [P, LT], F32)
        iota_x = sb("iota_x", [P, NX], F32)
        logits = sb("logits", [P, LT, NX], F32)
        shifted = sb("shifted", [P, LT, NX], F32)
        neg_top = sb("neg_top", [P, LT], F32)
        exps = sb("exps", [P, LT, NX], F32)
        exp_sum = sb("exp_sum", [P, LT], F32)
        sum_inv = sb("sum_inv", [P, LT], F32)
        route_probs = sb("route_probs", [P, LT, NX], F32)
        top = sb("top", [P, LT, TOP], F32)
        top_at = sb("top_at", [P, LT, TOP], U32)
        top_at_f = sb("top_at_f", [P, LT, 2], F32)
        picked = sb("picked", [P, 2, LT, NX], F32)
        gates = sb("gates", [P, 2, LT, NX], F32)
        gate_parts = sb("gate_parts", [P, LT, GATE_ROWS], F32R)
        gates_t = sb("gates_t", [GATE_ROWS, L], F32R)
        be_parts = sb("be_parts", [GATE_ROWS, D], F32R)

        scores_done = sem("scores_done")
        scores_read = sem("scores_read")
        max_ready = sem("max_ready")
        hi_ready = sem("hi_ready")
        split_ready = sem("split_ready")
        max_turned = sem("max_turned")
        max_copied = sem("max_copied")
        max_placed = sem("max_placed")
        keyed_done = sem("keyed_done")
        exp_done = sem("exp_done")
        out_done = sem("out_done")
        out_copied = sem("out_copied")
        out_turned = sem("out_turned")
        recip_ready = sem("recip_ready")
        out_ready = sem("out_ready")
        attn_stored = [sem(f"attn_stored{i}") for i in range(2)]

        raw_loaded = [sem(f"raw_loaded{i}") for i in range(RAW)]
        small_loaded = sem("small_loaded")
        bo_loaded = sem("bo_loaded")
        consts_ready = sem("consts_ready")
        x_loaded = sem("x2_loaded")
        attn_loaded = [sem(f"attn_loaded{i}") for i in range(2)]
        bias_added = sem("bias_added")
        w_hi = sem("w_hi")
        w_lo = sem("w_lo")
        at_done = sem("at_done")
        at_hi = sem("at_hi")
        at_lo = sem("at_lo")
        proj_done = sem("oproj_done")
        total_ready = sem("total_ready")
        stats_done = sem("stats2_done")
        moments_done = sem("moments2_done")
        eps_added = sem("eps2_added")
        rstd_ready = sem("rstd2_ready")
        norm_ready = sem("norm2_ready")
        x2_done = sem("x2_done")
        x2_hi = sem("x2_hi")
        x2_lo = sem("x2_lo")
        hidden_done = sem("hidden_done")
        hidden_ready = sem("hidden_ready")
        logits_done = sem("logits_done")
        logits_ready = sem("logits_ready")
        neg_top_ready = sem("neg_top_ready")
        shifted_ready = sem("shifted_ready")
        exps_ready = sem("exps_ready")
        sum_ready = sem("sum_ready")
        inv_ready = sem("inv_ready")
        probs_ready = sem("probs_ready")
        top_ready = sem("top_ready")
        at_ready = sem("at_ready")
        at_f_ready = sem("at_f_ready")
        picked_ready = sem("picked_ready")
        gates_ready = sem("gates_ready")
        gates_turned = sem("gates_turned")
        gates_copied = sem("gates_copied")
        be_zeroed = sem("be_zeroed")
        parts_zeroed = sem("parts_zeroed")
        be_hi = sem("be_hi")
        be_lo = sem("be_lo")
        gate_hi = sem("gate_hi")
        gate_split = sem("gate_split")
        bias_done = sem("bias_done")
        bias_in = sem("bias_in")
        expert_done = sem("expert_done")
        expert_in = sem("expert_in")
        out_stored = sem("out_stored")

        KEYED, MAXB, OUTB = 0, 4, 7
        TURN_OUT, TURN_MAX = LAG, 5
        EXTRAS = (0, TURN_OUT, TURN_MAX, ST - 1)
        FIRST = ITEMS * 3 // 2

        def slot(st, i):
            return MAXB + (4 * st + i + sum(e < st for e in EXTRAS)) % 3

        TURN_ATTENTION, PROJECT_OUT, TURN_NORM, HIDE = (2, 5), (2, 7), (3, 4), (3, 6)
        ROUNDED = ((1, 3), (1, 4), (2, 3))
        SMALL = 6

        def pairs(eng, one, first, last):
            if last - first == 1:
                one(first)
            else:
                with eng.Fori(first, last) as p:
                    one(p)

        block = ctx.enter_context(nc.Block())

        @block.gpsimd
        def _(pool):
            pool.wait_ge(bo_loaded, 16)
            nc.gpsimd.memset(be_raw[:], 0.0).then_inc(be_zeroed, 1)
            nc.gpsimd.memset(gate_parts[:].bitcast(F32), 0.0).then_inc(parts_zeroed, 1)
            nc.gpsimd.memset(minus_half2[:], -0.5).then_inc(consts_ready, 1)
            nc.gpsimd.iota(iota_x[:], pattern=[[1, NX]], base=0, channel_multiplier=0,
                           allow_small_or_imprecise_dtypes=True).then_inc(consts_ready, 1)
            pool.wait_ge(consts_ready, 2)

            def add_bias(c):
                pool.wait_ge(x_loaded, 16 * (c + 1))
                wait(pool, total_ready, 2 * c)
                nc.gpsimd.tensor_tensor(x_bias[:], x_again[:],
                                        bo_row[:].unsqueeze(1).to_broadcast([P, LT, D]), ALU.add).then_inc(bias_added, 1)

            def split_weights(p):
                pool.wait_ge(w_hi, p + 1)
                nc.gpsimd.tensor_tensor(w_t[:, p, LO], w_raw[:, p % RAW].rearrange("p k i o -> p k (i o)"),
                                        w_t[:, p, HI].bitcast(F32), ALU.subtract).then_inc(w_lo, 1)

            def invert(c):
                pool.wait_ge(eps_added, c + 1)
                nc.gpsimd.tensor_tensor(rstd2[:], var2[:], minus_half2[:], ALU.pow).then_inc(rstd_ready, 1)

            pool.wait_ge(be_hi, 1)
            nc.gpsimd.tensor_tensor(be_parts[2 * STEP:], be_raw[2 * STEP:], be_parts[2 * STEP:].bitcast(F32),
                                    ALU.subtract).then_inc(be_lo, 1)
            pool.wait_ge(be_lo, 1)
            split_weights(0)
            split_weights(1)
            add_bias(0)
            split_weights(2)
            invert(0)
            add_bias(1)
            for p in range(RAW, PAIRS // 2):
                split_weights(p)
            invert(1)
            for p in range(PAIRS // 2, PAIRS):
                split_weights(p)
                if p == PAIRS // 2:
                    add_bias(2)
            for c in range(2, B):
                invert(c)
                if c + 1 < B:
                    add_bias(c + 1)

        @block.sync
        def _(sp):
            def place_max(count, g):
                sp.wait_ge(max_copied, count)
                for part in range(2):
                    sp.dma_start(q_stack[MROW + part:MROW + part + 1, g, :, :].bitcast(F32),
                                 max_rows[part * GH * LT:(part + 1) * GH * LT, :]).then_inc(max_placed, 16)

            def load_attn(c):
                for i in range(2):
                    sp.wait_ge(attn_stored[i], 16 * NG // 2 * (c + 1))
                wait(sp, at_done, KC * (c - 1))
                sp.dma_start(attn[c % 2][:], attn_rows[c].rearrange("(t p) d -> p t d", p=P)).then_inc(
                    attn_loaded[c % 2], 16)

            def load_x(c):
                wait(sp, bias_added, c)
                sp.dma_start(x_again[:], x[c].rearrange("(t p) d -> p t d", p=P)).then_inc(x_loaded, 16)

            def load_weights(p):
                sp.wait_ge(w_lo, p - RAW + 1)
                load_pair(sp, we, w_raw, raw_loaded, p)

            for g in range(1, NG):
                load_stack(sp, 0, g)
            wait_stored(sp, B)
            sp.dma_start(bo_row[:], bo.partition_broadcast(P)).then_inc(bo_loaded, 16)
            place_max(1, 0)
            for p in range(RAW):
                load_pair(sp, we, w_raw, raw_loaded, p)
            load_x(0)
            sp.dma_start(bg1_col[:], bg1.rearrange("(h o) -> h o", o=1),
                         allow_slow_non_contiguous=True).then_inc(small_loaded, 16)
            sp.dma_start(wg2_sb[:], wg2[:, 0:NX]).then_inc(small_loaded, 16)
            sp.dma_start(bg2_row[:], bg2[0:NX].partition_broadcast(P)).then_inc(small_loaded, 16)
            sp.wait_ge(be_zeroed, 1)
            for n in range(3):
                sp.dma_start(be_raw[n * STEP:n * STEP + NX, :], be).then_inc(small_loaded, 16)

            def batch(b, last):
                for g in range(NG):
                    if last and g == 2:
                        sp.wait_ge(out_done, ST * (NG * b + 2))
                        load_attn(0)
                        load_weights(RAW)
                        load_weights(RAW + 1)
                    if not (last and g == NG - 1):
                        place_max(NG * b + g + 2, (g + 1) % NG)
                    if not last:
                        sp.wait_ge(out_done, ST * (NG * b + g + 1))
                        load_stack(sp, b + 1, g)
                    if last and g == NG - 1:
                        load_attn(1)
                        load_x(1)
                    sp.wait_ge(out_ready, NG * b + g + 1)
                    rows = attn_rows[b].rearrange("l d -> (l d)").rearrange(
                        "(h p x) -> p h x", h=H, p=P)[:, g * GH:(g + 1) * GH, :]
                    sp.dma_start(rows, attn_out[:, g % 2].rearrange("p j t e -> p j (t e)")).then_inc(
                        attn_stored[g % 2], 16)

            batch(0, False)
            with sp.Fori(1, B - 1) as b:
                batch(b, False)
            batch(B - 1, True)
            load_attn(2)
            load_weights(RAW + 2)
            load_x(2)
            load_weights(RAW + 3)
            load_attn(3)
            for p in range(RAW + 4, PAIRS):
                load_weights(p)
            load_x(3)
            for c in range(B):
                sp.wait_ge(expert_in, PER * PAIRS * (c + 1))
                sp.dma_start(out[c].rearrange("(t p) d -> p t d", p=P),
                             total[:, LT * c:LT * (c + 1), :]).then_inc(out_stored, 16)
            sp.wait_ge(out_stored, 16 * B)

        @block.scalar
        def _(act):
            def copy_max(count, bank):
                act.wait_ge(max_turned, count)
                wait(act, max_placed, 32 * (count - 1))
                nc.scalar.activation(max_rows[:], psum[0:2 * GH * LT, bank, 0:P], ACT.Copy).then_inc(max_copied, 1)

            def copy_out(count):
                act.wait_ge(out_done, ST * count)
                wait(act, out_turned, count - 1)
                nc.scalar.activation(o_raw[:], psum[:, OUTB, :], ACT.Copy).then_inc(out_copied, 1)

            def batch(b, first, last):
                for g in range(NG):
                    for st in range(ST):
                        step = ST * (NG * b + g) + st
                        for i in range(2):
                            act.wait_ge(keyed_done, 2 * step + i + 1)
                            if i == 0:
                                wait(act, out_done, step - PB + 1)
                            nc.scalar.activation(
                                probs[:, st % PB, 2 * i:2 * i + 2, :], psum[:, KEYED + 2 * i:KEYED + 2 * i + 2, :],
                                ACT.Exp, scale=SCALE).then_inc(exp_done, 1)
                        if st == LAG - 1 and not (first and g == 0):
                            copy_out(NG * b + g)
                        if st == TURN_MAX and not (last and g == NG - 1):
                            copy_max(NG * b + g + 2, slot(TURN_MAX, 4))
                        if last and (g, st) in ROUNDED:
                            round_weights(ROUNDED.index((g, st)))

            def round_weights(p):
                act.wait_ge(raw_loaded[p % RAW], 32 * (p // RAW + 1))
                act.wait_ge(out_done, ST * (NG * (B - 1) + min(p // PER_GROUP + 1, NG)))
                nc.scalar.activation(w_t[:, p, HI], w_raw[:, p % RAW].rearrange("p k i o -> p k (i o)"),
                                     ACT.Copy).then_inc(w_hi, 1)

            def round_attention(c):
                wait(act, proj_done, 2 * c)
                for k in range(KC):
                    act.wait_ge(at_done, KC * c + k + 1)
                    nc.scalar.activation(attn_t[:, HI, k, :], psum[:, TURNED + k, :], ACT.Copy).then_inc(at_hi, 1)

            def round_norm(c):
                wait(act, expert_done, LT * PAIRS * (c - 1))
                wait(act, hidden_done, c - 1)
                for k in range(KC):
                    act.wait_ge(x2_done, KC * c + k + 1)
                    nc.scalar.activation(x2_t[c % 2][:, HI, k, :], psum[:, TURNED + k, :], ACT.Copy).then_inc(x2_hi, 1)

            def gelu(c):
                act.wait_ge(hidden_done, c + 1)
                wait(act, logits_done, c)
                nc.scalar.activation(hidden[:], psum[0:HID, SUMS[0], :], ACT.Gelu,
                                     bias=bg1_col[:]).then_inc(hidden_ready, 1)

            def exp(c):
                act.wait_ge(shifted_ready, c + 1)
                nc.scalar.activation(exps[:], shifted[:], ACT.Exp).then_inc(exps_ready, 1)

            def copy_gates(c):
                act.wait_ge(gates_turned, c + 1)
                wait(act, bias_done, 2 * c)
                nc.scalar.activation(gates_t[:], psum[0:GATE_ROWS, TURNED, :], ACT.Copy).then_inc(gates_copied, 1)

            copy_max(1, KEYED)
            batch(0, True, False)
            with act.Fori(1, B - 1) as b:
                batch(b, False, False)
            act.wait_ge(small_loaded, 16 * SMALL)
            nc.scalar.activation(be_parts[:], be_raw[:], ACT.Copy).then_inc(be_hi, 1)
            batch(B - 1, False, True)
            gelu(0)
            copy_out(NG * B)
            exp(0)
            round_weights(RAW)
            copy_gates(0)
            for c in range(1, B):
                round_attention(c)
                if c == 1:
                    round_weights(4)
                    round_weights(5)
                round_norm(c)
                if c == 1:
                    round_weights(6)
                    round_weights(7)
                gelu(c)
                if c == 1:
                    for p in range(8, PAIRS):
                        round_weights(p)
                exp(c)
                copy_gates(c)

        @block.vector
        def _(dve):
            def reduce(n, group, i, bank):
                dve.wait_ge(scores_done, n + 1)
                nc.vector.tensor_reduce(max_part[:, group % 2, i // 2 % GH, i // 8, i % 2:i % 2 + 1],
                                        psum[:, bank, :], AX_X, ALU.max).then_inc(scores_read, 1)

            def split_max(count, group):
                dve.wait_ge(scores_read, ITEMS * count)
                nc.vector.tensor_reduce(neg_max[:], max_part[:, group % 2], AX_X, ALU.max,
                                        negate=True).then_inc(max_ready, 1)
                dve.wait_ge(max_ready, count)
                wait(dve, max_turned, count - 1)
                nc.vector.tensor_copy(max_split[:, HI], neg_max[:]).then_inc(hi_ready, 1)
                dve.wait_ge(hi_ready, count)
                nc.vector.tensor_tensor(max_split[:, LO], neg_max[:], max_split[:, HI].bitcast(F32),
                                        ALU.subtract).then_inc(split_ready, 1)

            def normalise(count, b, g, bank):
                dve.wait_ge(out_turned, count)
                turned = psum[:, bank, :].rearrange("p (t j e) -> p t j e", t=LT, j=GH)
                nc.vector.reciprocal(recip[:], turned[:, :, :, E]).then_inc(recip_ready, 1)
                dve.wait_ge(recip_ready, count)
                wait(dve, attn_stored[g % 2], 16 * (NG // 2 * b + g // 2))
                dst = attn_out[:, g % 2].rearrange("p j t e -> p t j e")
                nc.vector.tensor_tensor(dst, turned[:, :, :, 0:E],
                                        recip[:].unsqueeze(3).to_broadcast([P, LT, GH, E]), ALU.mult).then_inc(out_ready, 1)

            def round_here(done, c, dst, hi_made):
                for k in range(KC):
                    dve.wait_ge(done, KC * c + k + 1)
                    nc.vector.tensor_copy(dst[:, HI, k, :], psum[:, TURNED + k, :]).then_inc(hi_made, 1)

            def split_attention(c):
                for k in range(KC):
                    dve.wait_ge(at_hi, KC * c + k + 1)
                    nc.vector.tensor_tensor(attn_t[:, LO, k, :], psum[:, TURNED + k, :],
                                            attn_t[:, HI, k, :].bitcast(F32), ALU.subtract).then_inc(at_lo, 1)

            def residual(c):
                dve.wait_ge(bias_added, c + 1)
                for h in range(2):
                    dve.wait_ge(proj_done, 2 * c + h + 1)
                    t = LT * c + 2 * h
                    nc.vector.tensor_tensor(total[:, t:t + 2, :],
                                            psum[:, (SUMS if c else FIRST_SUMS)[h], :].rearrange("p (t d) -> p t d", t=2),
                                            x_bias[:, 2 * h:2 * h + 2, :], ALU.add).then_inc(total_ready, 1)
                for t in range(LT):
                    dve.wait_ge(total_ready, 2 * c + t // 2 + 1)
                    nc.vector.bn_stats(stats2[:, t, :], total[:, LT * c + t, :]).then_inc(stats_done, 1)
                for t in range(LT):
                    dve.wait_ge(stats_done, LT * c + t + 1)
                    nc.vector.bn_aggr(moments2[:, t, :], stats2[:, t, :]).then_inc(moments_done, 1)
                dve.wait_ge(moments_done, LT * (c + 1))
                nc.vector.tensor_scalar(var2[:], moments2[:, :, 1], EPS, None, ALU.add).then_inc(eps_added, 1)

            def norm(c):
                dve.wait_ge(rstd_ready, c + 1)
                wait(dve, x2_done, KC * c)
                for t in range(LT):
                    nc.vector.tensor_scalar(x2_norm[:, t, :], total[:, LT * c + t, :], moments2[:, t, 0:1],
                                            rstd2[:, t:t + 1], ALU.subtract, ALU.mult).then_inc(norm_ready, 1)

            def split_norm(c):
                for k in range(KC):
                    dve.wait_ge(x2_hi, KC * c + k + 1)
                    nc.vector.tensor_tensor(x2_t[c % 2][:, LO, k, :], psum[:, TURNED + k, :],
                                            x2_t[c % 2][:, HI, k, :].bitcast(F32), ALU.subtract).then_inc(x2_lo, 1)

            def route(c):
                dve.wait_ge(logits_done, c + 1)
                nc.vector.tensor_tensor(logits[:], psum[:, LOGITS, 0:LT * NX].rearrange("p (t x) -> p t x", t=LT),
                                        bg2_row[:].unsqueeze(1).to_broadcast([P, LT, NX]),
                                        ALU.add).then_inc(logits_ready, 1)
                dve.wait_ge(logits_ready, c + 1)
                nc.vector.tensor_reduce(neg_top[:], logits[:], AX_X, ALU.max, negate=True).then_inc(neg_top_ready, 1)
                dve.wait_ge(neg_top_ready, c + 1)
                nc.vector.tensor_tensor(shifted[:], logits[:], neg_top[:].unsqueeze(2).to_broadcast([P, LT, NX]),
                                        ALU.add).then_inc(shifted_ready, 1)

            def choose(c):
                dve.wait_ge(exps_ready, c + 1)
                nc.vector.tensor_reduce(exp_sum[:], exps[:], AX_X, ALU.add).then_inc(sum_ready, 1)
                dve.wait_ge(sum_ready, c + 1)
                nc.vector.reciprocal(sum_inv[:], exp_sum[:]).then_inc(inv_ready, 1)
                dve.wait_ge(inv_ready, c + 1)
                nc.vector.tensor_tensor(route_probs[:], exps[:], sum_inv[:].unsqueeze(2).to_broadcast([P, LT, NX]),
                                        ALU.mult).then_inc(probs_ready, 1)
                dve.wait_ge(probs_ready, c + 1)
                for t in range(LT):
                    nc.vector.max(top[:, t, :], route_probs[:, t, :]).then_inc(top_ready, 1)
                for t in range(LT):
                    dve.wait_ge(top_ready, LT * c + t + 1)
                    nc.vector.max_index(top_at[:, t, :], top[:, t, :], route_probs[:, t, :]).then_inc(at_ready, 1)

            def make_gates(c):
                dve.wait_ge(at_ready, LT * (c + 1))
                nc.vector.tensor_copy(top_at_f[:], top_at[:, :, 0:2]).then_inc(at_f_ready, 1)
                dve.wait_ge(at_f_ready, c + 1)
                for i in range(2):
                    for t in range(LT):
                        nc.vector.tensor_scalar(picked[:, i, t, :], iota_x[:], top_at_f[:, t, i:i + 1],
                                                top[:, t, i:i + 1], ALU.is_equal, ALU.mult).then_inc(picked_ready, 1)
                dve.wait_ge(picked_ready, 2 * LT * (c + 1))
                nc.vector.tensor_tensor(gates[:, c % 2], picked[:, 0], picked[:, 1], ALU.add).then_inc(gates_ready, 1)
                dve.wait_ge(gates_ready, c + 1)
                wait(dve, gates_turned, c)
                for n in (0, 2):
                    nc.vector.tensor_copy(gate_parts[:, :, n * STEP:n * STEP + NX], gates[:, c % 2]).then_inc(gate_hi, 1)
                dve.wait_ge(gate_hi, 2 * c + 1)
                nc.vector.tensor_tensor(gate_parts[:, :, STEP:STEP + NX], gates[:, c % 2],
                                        gate_parts[:, :, 0:NX].bitcast(F32), ALU.subtract).then_inc(gate_split, 1)

            def add_biases(c):
                if c == 0:
                    dve.wait_ge(expert_in, PER)
                for h in range(2):
                    dve.wait_ge(bias_done, 2 * c + h + 1)
                    t = LT * c + 2 * h
                    nc.vector.tensor_tensor(total[:, t:t + 2, :], total[:, t:t + 2, :],
                                            psum[:, SUMS[h], :].rearrange("p (t d) -> p t d", t=2),
                                            ALU.add).then_inc(bias_in, 1)

            def experts(c, p):
                if isinstance(p, int) and p == 0:
                    dve.wait_ge(gates_ready, c + 1)
                before = PER * (PAIRS * c + p)
                for t in range(0, LT, 2):
                    for e in range(2):
                        for u in (t, t + 1):
                            if e == 0:
                                dve.wait_ge(expert_done, LT * (PAIRS * c + p) + u + 1)
                            wait(dve, expert_in, before + 2 * t + (u - t) + 1 - (0 if e else PER - 2))
                            nc.vector.scalar_tensor_tensor(
                                out=total[:, LT * c + u, :], in0=psum[:, EXPERT + u, e * D:(e + 1) * D],
                                scalar=gates[:, c % 2, u, bass.ds(2 * p + e, 1)], in1=total[:, LT * c + u, :],
                                op0=ALU.mult, op1=ALU.add).then_inc(expert_in, 1)

            for i in range(ITEMS):
                reduce(i, 0, i, MAXB + i % 3)
            split_max(1, 0)
            for i in range(ITEMS // 2):
                reduce(ITEMS + i, 1, i, MAXB + (ITEMS + i) % 3)

            def batch(b, first, last):
                for g in range(NG):
                    for st in range(ST):
                        step, step_in = ST * (NG * b + g) + st, ST * g + st
                        ahead = 1 if st < ST // 2 else 2
                        if not (last and g + ahead >= NG):
                            for i in range(4):
                                reduce(FIRST + 4 * step + i, g + ahead, (FIRST + 4 * step_in + i) % ITEMS, slot(st, i))
                        if st == TURN_OUT and not (first and g == 0):
                            normalise(NG * b + g, b, g - 1, slot(TURN_OUT, 4))
                        if st == 3 and not (last and g == NG - 1):
                            split_max(NG * b + g + 2, g + 1)
                        if last and (g, st) == TURN_ATTENTION:
                            round_here(at_done, 0, attn_t, at_hi)
                            split_attention(0)
                        if last and (g, st) == PROJECT_OUT:
                            residual(0)
                            norm(0)
                        if last and (g, st) == TURN_NORM:
                            round_here(x2_done, 0, x2_t[0], x2_hi)
                            split_norm(0)

            batch(0, True, False)
            with dve.Fori(1, B - 1) as b:
                batch(b, False, False)
            dve.wait_ge(small_loaded, 16 * SMALL)
            dve.wait_ge(consts_ready, 2)
            dve.wait_ge(parts_zeroed, 1)
            batch(B - 1, False, True)
            route(0)
            choose(0)
            make_gates(0)
            for c in range(B):
                ahead = c + 1 < B
                def run(first, last):
                    pairs(dve, lambda p: experts(c, p), first, last)
                if c == 0:
                    run(0, 1)
                    normalise(NG * B, B, -1, SUMS[0])
                    add_biases(0)
                    dve.wait_ge(bias_in, 2)
                    split_attention(1)
                    run(1, 2)
                else:
                    if ahead:
                        split_attention(c + 1)
                    dve.wait_ge(bias_in, 2 * (c + 1))
                    run(0, 1)
                    run(1, 2)
                if not ahead:
                    run(2, PAIRS)
                    continue
                residual(c + 1)
                run(2, 3)
                norm(c + 1)
                run(3, 4)
                split_norm(c + 1)
                run(4, 6)
                route(c + 1)
                run(6, 7)
                choose(c + 1)
                run(7, 8)
                make_gates(c + 1)
                run(8, PAIRS)
                add_biases(c + 1)

        @block.tensor
        def _(pe):
            def scores(g, i, bank):
                t, j, half = i // 8, i // 2 % GH, i % 2
                nc.tensor.matmul(psum[:, bank, :], q_stack[:, g, j, t * P:(t + 1) * P],
                                 k_stack[:, g, j, half * 512:(half + 1) * 512], start=True,
                                 stop=True).then_inc(scores_done, 1)

            def turn_max(count, bank):
                pe.wait_ge(split_ready, count)
                nc.tensor.transpose(psum[0:2 * GH * LT, bank, 0:P], max_split[:].rearrange(
                    "p a j t -> p (a j t)").bitcast(F32), ident[:]).then_inc(max_turned, 1)

            def turn_out(count, bank):
                pe.wait_ge(out_copied, count)
                queries = o_raw[:].rearrange("c (p t) -> c p t", t=LT)
                for t in range(LT):
                    last = nc.tensor.transpose(psum[:, bank, t * P:(t + 1) * P], queries[:, :, t], ident[:])
                last.then_inc(out_turned, 1)

            def keyed(step, g, st, i):
                if not (isinstance(step, int) and step == 0):
                    pe.wait_ge(exp_done, 2 * step + i - 1)
                for j in (2 * i, 2 * i + 1):
                    last = nc.tensor.matmul(psum[:, KEYED + j, :], k_stack[:, g, j, st * P:(st + 1) * P],
                                            q_stack[:, g, j, :], start=True, stop=True)
                last.then_inc(keyed_done, 1)

            def weigh(step, g, st):
                pe.wait_ge(exp_done, 2 * (step + 1))
                for j in range(GH):
                    last = nc.tensor.matmul(psum[32 * j:32 * j + VW, OUTB, :], v_stack[:, g, st, j * VW:(j + 1) * VW],
                                            probs[:, st % PB, j, :], start=(st == 0), stop=(st == ST - 1),
                                            skip_group_check=True)
                last.then_inc(out_done, 1)

            def turn_attention(c):
                pe.wait_ge(attn_loaded[c % 2], 16 * (c // 2 + 1))
                if c == 0:
                    pe.wait_ge(scores_read, ITEMS * NG * B)
                    pe.wait_ge(out_ready, NG * B - 2)
                wait(pe, gates_copied, c)
                wait(pe, logits_ready, c)
                for k in range(KC):
                    for t in range(LT):
                        last = nc.tensor.transpose(psum[:, TURNED + k, t * P:(t + 1) * P],
                                                   attn[c % 2][:, t, k * P:(k + 1) * P], ident[:])
                    last.then_inc(at_done, 1)

            def project_out(c):
                pe.wait_ge(at_lo, KC * (c + 1))
                for h in range(2):
                    if c == 0:
                        pe.wait_ge(max_copied, NG * B)
                    wait(pe, bias_in, 2 * (c - 1) + h + 1)
                    for u in range(2):
                        t = 2 * h + u
                        for m, (a, w, k) in enumerate(TERMS):
                            last = nc.tensor.matmul(psum[:, (SUMS if c else FIRST_SUMS)[h], u * D:(u + 1) * D],
                                                    attn_t[:, a, k, t * P:(t + 1) * P], wo_t[:, w, k, :],
                                                    start=(m == 0), stop=(m == len(TERMS) - 1))
                    last.then_inc(proj_done, 1)

            def turn_norm(c):
                pe.wait_ge(norm_ready, LT * (c + 1))
                if c == 0:
                    pe.wait_ge(out_ready, NG * B - 1)
                for k in range(KC):
                    for t in range(LT):
                        last = nc.tensor.transpose(psum[:, TURNED + k, t * P:(t + 1) * P],
                                                   x2_norm[:, t, k * P:(k + 1) * P], ident[:])
                    last.then_inc(x2_done, 1)

            def hide(c):
                pe.wait_ge(x2_lo, KC * (c + 1))
                for m, (a, w, k) in enumerate(TERMS):
                    last = nc.tensor.matmul(psum[:, SUMS[0], :], wg1_t[:, w, k, :], x2_t[c % 2][:, a, k, :],
                                            start=(m == 0), stop=(m == len(TERMS) - 1))
                last.then_inc(hidden_done, 1)

            def score(c):
                pe.wait_ge(hidden_ready, c + 1)
                for t in range(LT):
                    last = nc.tensor.matmul(psum[:, LOGITS, t * NX:(t + 1) * NX], hidden[:, t * P:(t + 1) * P],
                                            wg2_sb[:], start=True, stop=True)
                last.then_inc(logits_done, 1)

            def turn_gates(c):
                pe.wait_ge(gate_hi, 2 * (c + 1))
                pe.wait_ge(gate_split, c + 1)
                for t in range(LT):
                    last = nc.tensor.transpose(psum[0:GATE_ROWS, TURNED, t * P:(t + 1) * P],
                                               gate_parts[:, t, :].bitcast(F32), ident[:])
                last.then_inc(gates_turned, 1)

            def bias(c):
                pe.wait_ge(gates_copied, c + 1)
                if c == 0:
                    pe.wait_ge(be_lo, 1)
                    pe.wait_ge(out_ready, NG * B)
                for h in range(2):
                    for u in range(2):
                        t = 2 * h + u
                        last = nc.tensor.matmul(psum[:, SUMS[h], u * D:(u + 1) * D], gates_t[:, t * P:(t + 1) * P],
                                                be_parts[:], start=True, stop=True)
                    last.then_inc(bias_done, 1)

            def experts(c, p):
                if c == 0:
                    pe.wait_ge(w_lo, p + 1)
                for t in range(LT):
                    wait(pe, expert_in, PER * (PAIRS * c + p - 1) + 4 * (t // 2 + 1))
                    for m, (a, w, k) in enumerate(TERMS):
                        last = nc.tensor.matmul(psum[:, EXPERT + t, :], x2_t[c % 2][:, a, k, t * P:(t + 1) * P],
                                                w_t[:, bass.ds(p, 1), w, k, :], start=(m == 0),
                                                stop=(m == len(TERMS) - 1))
                    last.then_inc(expert_done, 1)

            pe.wait_ge(stack_loaded[0], 16 * LOADS)
            nc.tensor.matmul(psum[:, OUTB, :], q_stack[:, 0, 0, 0:P], q_stack[:, 0, 0, :], start=True, stop=True)
            for i in range(ITEMS):
                wait(pe, scores_read, i - 2)
                scores(0, i, MAXB + i % 3)
            pe.wait_ge(stack_loaded[1], 16 * LOADS)
            for i in range(ITEMS // 2):
                if i == 3:
                    turn_max(1, KEYED)
                pe.wait_ge(scores_read, ITEMS + i - 2)
                scores(1, i, MAXB + (ITEMS + i) % 3)

            def batch(b, first, last):
                for g in range(NG):
                    for st in range(ST):
                        step = ST * (NG * b + g) + st
                        if st == 0:
                            pe.wait_ge(max_placed, 32 * (NG * b + g + 1))
                        ahead = 1 if st < ST // 2 else 2
                        maxima = not (last and g + ahead >= NG)
                        if maxima and st == ST // 2:
                            pe.wait_ge(stack_loaded[(g + 2) % NG], 16 * LOADS * (b + 1 + (g + 2) // NG))

                        def item(i):
                            if not maxima:
                                return
                            n = FIRST + 4 * step + i
                            if (st - 1) % ST in EXTRAS and i < 2:
                                pe.wait_ge(scores_read, n - 1)
                            elif (st - 1) % ST in EXTRAS and i == 2:
                                if st == TURN_OUT + 1:
                                    wait(pe, out_ready, NG * b + g)
                                if st == TURN_MAX + 1:
                                    pe.wait_ge(max_copied, NG * b + g + 2)
                            else:
                                pe.wait_ge(scores_read, n - 2)
                            scores((g + ahead) % NG, (FIRST + 4 * (ST * g + st) + i) % ITEMS, slot(st, i))

                        keyed(step, g, st, 0)
                        item(0)
                        keyed(step, g, st, 1)
                        item(1)
                        item(2)
                        if not (first and g == 0 and st < LAG):
                            if st == LAG:
                                wait(pe, out_copied, NG * b + g)
                            weigh(step - LAG, (g if st >= LAG else g - 1) % NG, (st - LAG) % ST)
                        item(3)
                        if st == TURN_OUT and not (first and g == 0):
                            if maxima:
                                pe.wait_ge(scores_read, FIRST + 4 * step + 2)
                            else:
                                pe.wait_ge(out_ready, NG * b + g - 1)
                            turn_out(NG * b + g, slot(TURN_OUT, 4))
                        if st == TURN_MAX and not (last and g == NG - 1):
                            if maxima:
                                pe.wait_ge(scores_read, FIRST + 4 * step + 2)
                            turn_max(NG * b + g + 2, slot(TURN_MAX, 4))
                        if last and (g, st) == TURN_ATTENTION:
                            turn_attention(0)
                        if last and (g, st) == PROJECT_OUT:
                            project_out(0)
                        if last and (g, st) == TURN_NORM:
                            turn_norm(0)
                        if last and (g, st) == HIDE:
                            hide(0)

            batch(0, True, False)
            with pe.Fori(1, B - 1) as b:
                batch(b, False, False)
            batch(B - 1, False, True)
            for lag in range(LAG, 0, -1):
                weigh(ST * NG * B - lag, NG - 1, ST - lag)
            score(0)
            for c in range(B):
                ahead = c + 1 < B
                def run(first, last):
                    pairs(pe, lambda p: experts(c, p), first, last)
                if c == 0:
                    run(0, 1)
                    turn_out(NG * B, SUMS[0])
                    turn_gates(0)
                    bias(0)
                    turn_attention(1)
                    run(1, 2)
                else:
                    if ahead:
                        turn_attention(c + 1)
                    run(0, 2)
                if not ahead:
                    run(2, PAIRS)
                    continue
                project_out(c + 1)
                run(2, 4)
                turn_norm(c + 1)
                run(4, 5)
                hide(c + 1)
                run(5, 6)
                score(c + 1)
                run(6, 9)
                turn_gates(c + 1)
                run(9, PAIRS)
                bias(c + 1)


_INS = ['x', 'ctx_1024', 'L0_xattn_Wq', 'L0_xattn_bq', 'L0_xattn_Wo', 'L0_xattn_bo', 'L0_ffn_wg1', 'L0_ffn_bg1',
        'L0_ffn_wg2', 'L0_ffn_bg2', 'L0_ffn_We', 'L0_ffn_be']
_OUT = ((B, L, D), 'float32')


def kernel(**inputs):
    import numpy as _np
    import concourse.bacc as _bacc
    from concourse import mybir as _mybir
    from concourse.bass_utils import run_bass_kernel_spmd as _run

    nc = _bacc.Bacc("TRN2", target_bir_lowering=False, num_devices=1)
    arrays, args = {}, []
    for name in _INS:
        a = _np.ascontiguousarray(inputs[name])
        arrays[f"in_{name}_dram"] = a
        args.append(nc.dram_tensor(f"in_{name}_dram", a.shape, _mybir.dt.from_np(a.dtype), kind="ExternalInput").ap())
    args.append(nc.dram_tensor("out_dram", _OUT[0], _mybir.dt.from_np(_np.dtype(_OUT[1])), kind="ExternalOutput").ap())
    mixed_kernel(nc, *args)
    r = _run(nc, [arrays], core_ids=[0])
    return r.results[0]["out_dram"]
```
